# Optimizing a Trainium2 kernel written in Bass

```python
import numpy as np
import jax
import jax.numpy as jnp

def _softmax(x, axis=-1):
    return jax.nn.softmax(x, axis=axis)

def _gelu(x):
    return jax.nn.gelu(x, approximate=True)

def _silu(x):
    return jax.nn.silu(x)

def _sigmoid(x):
    return jax.nn.sigmoid(x)

def _layernorm(x, axis=-1, eps=1e-05):
    m = jnp.mean(x, axis=axis, keepdims=True)
    v = jnp.var(x, axis=axis, keepdims=True)
    return (x - m) / jnp.sqrt(v + eps)

def _scatter_add(tgt, idx, src, axis=0):
    return tgt.at[idx].add(src)

def _segment_sum(src, seg, n):
    return jax.ops.segment_sum(src, seg, n)
kernel_name = 'mk_adj_resnorm_d1_adj_r2_04b736'

def setup_inputs(seed: int=0):
    np.random.seed(seed)
    _w = jnp.asarray

    def _rec_inputs():
        import jax
        import jax.numpy as jnp
        _gk = jax.random.key(seed)
        x = 7.22e-05 + 1 * jax.random.normal(jax.random.fold_in(_gk, 1), (16, 512, 256), jnp.float32)
        _w = (1.0 + jnp.arange(512, dtype=jnp.float32)) ** (-0.5)
        _w = _w / _w.mean()
        _pij = jnp.clip(0.00390625 * _w[:, None] * _w[None, :], 0.0, 1.0)
        _a = jax.random.uniform(jax.random.fold_in(_gk, 2), (512, 512)) < _pij
        _a = jnp.logical_or(_a, jnp.swapaxes(_a, -1, -2))
        _a = jnp.logical_or(_a, jnp.eye(512, dtype=bool))
        _af = _a.astype(jnp.float32)
        _af = _af * jax.random.uniform(jax.random.fold_in(_gk, 3), (512, 512), jnp.float32, 0.05, 0.00390622)
        adj = _af
        return (x, adj)
    x, adj = _rec_inputs()

    def _L0_gnn_setup():
        import jax, jax.numpy as jnp
        import numpy as np
        B, N, D, T = (64, 128, 256, 3)

        def _lin(v, W, b):
            return jnp.einsum('...i,oi->...o', v, W) + b
        key = jax.random.key(seed)
        ks = jax.random.split(key, 12)
        s2 = 1.0 / np.sqrt(2 * D)
        s1 = 1.0 / np.sqrt(D)
        return {'x': jax.random.normal(ks[0], (B, N, D), jnp.float32), 'in_mat': jax.random.uniform(ks[1], (N, N), jnp.float32) / N, 'out_mat': jax.random.uniform(ks[2], (N, N), jnp.float32) / N, 'w3_w': jax.random.normal(ks[3], (D, 2 * D), jnp.float32) * s2, 'w3_b': jnp.zeros((D,), jnp.float32), 'u3_w': jax.random.normal(ks[4], (D, D), jnp.float32) * s1, 'u3_b': jnp.zeros((D,), jnp.float32), 'w4_w': jax.random.normal(ks[5], (D, 2 * D), jnp.float32) * s2, 'w4_b': jnp.zeros((D,), jnp.float32), 'w5_w': jax.random.normal(ks[6], (D, 2 * D), jnp.float32) * s2, 'w5_b': jnp.zeros((D,), jnp.float32), 'u5_w': jax.random.normal(ks[7], (D, D), jnp.float32) * s1, 'u5_b': jnp.zeros((D,), jnp.float32)}
    _L0_gnn_all = _L0_gnn_setup()
    _L0_gnn_in = {k: v for k, v in _L0_gnn_all.items() if k in ('w3_w', 'w3_b', 'u3_w', 'u3_b', 'w4_w', 'w4_b', 'w5_w', 'w5_b', 'u5_w', 'u5_b')}
    del _L0_gnn_all
    return {'x': x, 'adj': adj, 'L0_gnn_w3_w': _L0_gnn_in['w3_w'], 'L0_gnn_w3_b': _L0_gnn_in['w3_b'], 'L0_gnn_u3_w': _L0_gnn_in['u3_w'], 'L0_gnn_u3_b': _L0_gnn_in['u3_b'], 'L0_gnn_w4_w': _L0_gnn_in['w4_w'], 'L0_gnn_w4_b': _L0_gnn_in['w4_b'], 'L0_gnn_w5_w': _L0_gnn_in['w5_w'], 'L0_gnn_w5_b': _L0_gnn_in['w5_b'], 'L0_gnn_u5_w': _L0_gnn_in['u5_w'], 'L0_gnn_u5_b': _L0_gnn_in['u5_b']}

def reference(x, adj, L0_gnn_w3_w, L0_gnn_w3_b, L0_gnn_u3_w, L0_gnn_u3_b, L0_gnn_w4_w, L0_gnn_w4_b, L0_gnn_w5_w, L0_gnn_w5_b, L0_gnn_u5_w, L0_gnn_u5_b):
    import jax
    import jax.numpy as jnp

    def _L0_gnn_ref(x, in_mat, out_mat, w3_w, w3_b, u3_w, u3_b, w4_w, w4_b, w5_w, w5_b, u5_w, u5_b):
        import jax, jax.numpy as jnp
        import numpy as np
        B, N, D, T = (64, 128, 256, 3)

        def _lin(v, W, b):
            return jnp.einsum('...i,oi->...o', v, W) + b
        h = x
        for _ in range(T):
            a_in = jnp.einsum('nm,bmd->bnd', in_mat, h)
            a_out = jnp.einsum('nm,bmd->bnd', out_mat, h)
            av = jnp.concatenate([a_in, a_out], axis=-1)
            z = jax.nn.sigmoid(_lin(av, w3_w, w3_b) + _lin(h, u3_w, u3_b))
            r = jax.nn.sigmoid(_lin(av, w4_w, w4_b) + _lin(h, u3_w, u3_b))
            hv = jnp.tanh(_lin(av, w5_w, w5_b) + _lin(r * h, u5_w, u5_b))
            h = (1.0 - z) * h + z * hv
        return h
    x = _layernorm(x + _L0_gnn_ref(x, adj, adj, L0_gnn_w3_w, L0_gnn_w3_b, L0_gnn_u3_w, L0_gnn_u3_b, L0_gnn_w4_w, L0_gnn_w4_b, L0_gnn_w5_w, L0_gnn_w5_b, L0_gnn_u5_w, L0_gnn_u5_b), axis=-1)
    return x

_drawn_inputs = setup_inputs


def setup_inputs(seed=0):
    import zlib

    import numpy as np

    out = dict(_drawn_inputs(seed))
    spreads = {'L0_gnn_w3_b': (0.0, 0.462),
     'L0_gnn_u3_b': (0.0, 0.409),
     'L0_gnn_w4_b': (0.0, 0.8),
     'L0_gnn_w5_b': (0.0, 0.1),
     'L0_gnn_u5_b': (0.0, 0.1)}
    factors = {'L0_gnn_w3_w': 3.969, 'L0_gnn_w4_w': 8.0}
    for name, (base, spread) in spreads.items():
        noise = np.random.default_rng([zlib.crc32(name.encode()), seed]).standard_normal(out[name].shape)
        drawn = base * np.exp(spread * noise) if base else spread * noise
        out[name] = jnp.asarray(drawn.astype(out[name].dtype))
    for name, factor in factors.items():
        out[name] = (out[name] * factor).astype(out[name].dtype)
    return out
```

```python
from contextlib import ExitStack

import concourse.bass as bass
from concourse import mybir


def gated_graph_steps_kernel(nc: bass.Bass, x, adj, w3_w, w3_b, u3_w, u3_b, w4_w, w4_b,
                             w5_w, w5_b, u5_w, u5_b, out):
    F32 = mybir.dt.float32
    F32R = mybir.dt.float32r
    ALU = mybir.AluOpType
    ACT = mybir.ActivationFunctionType

    P = 128
    B, N, D = x.shape
    STEPS = 3
    SLOTS = 2
    PAIRS = B // SLOTS
    UNITS = STEPS * SLOTS
    NT = N // P
    DT = D // P
    HALVES = 2
    EPS = 1e-5
    LAST_STEP = UNITS - SLOTS
    assert NT == 2 * HALVES and DT == HALVES and N == 512 and PAIRS >= 2

    def half(p, k, j):
        return 2 * UNITS * p + (2 * k + j + 1)

    def part(p, s, j):
        return 2 * SLOTS * p + (2 * s + j + 1)

    def once(p, s):
        return SLOTS * p + (s + 1)

    def summed(p, s, j):
        return part(p + 1, s, j)

    def stored(p):
        return 16 * (p + 1)

    ctx = ExitStack()
    with ctx:
        def sb(name, shape, dt=F32):
            return ctx.enter_context(nc.sbuf_tensor(name, shape, dt))

        def sem(name):
            return ctx.enter_context(nc.semaphore(name))

        adjT_hi = sb("adjT_hi", [P, NT, N], F32R)
        adjT_lo = sb("adjT_lo", [P, NT, N], F32R)
        WEIGHTS = ("u3", "w4", "w3", "w5", "u5")
        wT_hi = {w: sb(f"{w}T_hi", [P, DT, D], F32R) for w in WEIGHTS}
        wT_lo = {w: sb(f"{w}T_lo", [P, DT, D], F32R) for w in WEIGHTS}
        BIASES = ("w3", "w4", "w5", "u3", "u5")
        bias_in = sb("bias_in", [P, len(BIASES), DT])
        bias = sb("bias", [P, 3, DT])
        ident = sb("ident", [P, P])
        minus_half = sb("minus_half", [P, NT])
        table_scratch = sb("table_scratch", [P, 1])

        x_in = [sb(f"x_in{s}", [P, NT, D]) for s in range(SLOTS)]
        x_res = [sb(f"x_res{s}", [P, NT, D]) for s in range(SLOTS)]
        nat_hi = [sb(f"nat_hi{s}", [P, NT, D], F32R) for s in range(SLOTS)]
        nat_lo = [sb(f"nat_lo{s}", [P, NT, D], F32R) for s in range(SLOTS)]
        hT = [sb(f"hT{s}", [P, DT, N]) for s in range(SLOTS)]
        hT_hi = [sb(f"hT_hi{s}", [P, DT, N], F32R) for s in range(SLOTS)]
        hT_lo = [sb(f"hT_lo{s}", [P, DT, N], F32R) for s in range(SLOTS)]
        y = [sb(f"y{s}", [P, NT, D]) for s in range(SLOTS)]
        stats = [sb(f"stats{s}", [P, NT, 6]) for s in range(SLOTS)]
        moments = [sb(f"moments{s}", [P, NT, 2]) for s in range(SLOTS)]
        var_eps = [sb(f"var_eps{s}", [P, NT]) for s in range(SLOTS)]
        rstd = [sb(f"rstd{s}", [P, NT]) for s in range(SLOTS)]

        aT_hi = sb("aT_hi", [P, DT, N], F32R)
        aT_lo = sb("aT_lo", [P, DT, N], F32R)
        u_sb = sb("u_sb", [P, DT, N])
        r_sb = sb("r_sb", [P, DT, N])
        z_sb = sb("z_sb", [P, DT, N])
        v_sb = sb("v_sb", [P, DT, N])
        rh = sb("rh", [P, DT, N])
        rh_hi = sb("rh_hi", [P, DT, N], F32R)
        rh_lo = sb("rh_lo", [P, DT, N], F32R)
        change = sb("change", [P, DT, N])

        adj_in = sb("adj_in", [P, NT, N])
        w_in = {"w3": v_sb, "w4": r_sb, "w5": z_sb,
                "u3": change[:, 0, :].rearrange("p (t d) -> p t d", t=DT),
                "u5": change[:, 1, :].rearrange("p (t d) -> p t d", t=DT)}
        w_sum = {"w4": rh[:, 0, :].rearrange("p (t d) -> p t d", t=DT),
                 "w3": rh[:, 1, :].rearrange("p (t d) -> p t d", t=DT),
                 "w5": u_sb[:, 0, :].rearrange("p (t d) -> p t d", t=DT)}
        w_nat = {**w_sum, "u3": w_in["u3"], "u5": w_in["u5"]}

        banks = [ctx.enter_context(nc.psum_tensor(f"bank{i}", [P, N], F32)) for i in range(8)]
        ut_bank, ra_bank, z_bank, v_bank = banks[0:2], banks[2:4], banks[4:6], banks[6:8]
        PREP = [("adj", 0, 4), ("adj", 1, 5), ("adj", 2, 6), ("adj", 3, 7),
                ("u3", 0, 4), ("w4", 0, 5), ("w3", 0, 6), ("w5", 0, 7), ("u5", 0, 0)]

        x_loaded = [sem(f"x_loaded{s}") for s in range(SLOTS)]
        y_stored = [sem(f"y_stored{s}") for s in range(SLOTS)]
        adj_loaded = sem("adj_loaded")
        w_loaded = {w: sem(f"{w}_loaded") for w in WEIGHTS}
        bias_loaded = sem("bias_loaded")
        prep_done = sem("prep_done")
        u_done = sem("u_done")
        r_done = sem("r_done")
        z_done = sem("z_done")
        v_done = sem("v_done")
        a_done = sem("a_done")
        t_done = sem("t_done")
        xt_done = sem("xt_done")
        prep_hi = sem("prep_hi")
        u_copied = sem("u_copied")
        r_ready = sem("r_ready")
        z_ready = sem("z_ready")
        v_ready = sem("v_ready")
        rh_hi_ready = sem("rh_hi_ready")
        h_hi_ready = sem("h_hi_ready")
        nat_hi_ready = sem("nat_hi_ready")
        a_hi_ready = sem("a_hi_ready")
        xt_copied = sem("xt_copied")
        x_res_ready = sem("x_res_ready")
        w_added = sem("w_added")
        prep_lo = sem("prep_lo")
        bias_ready = sem("bias_ready")
        r_summed = sem("r_summed")
        z_summed = sem("z_summed")
        rh_ready = sem("rh_ready")
        rh_lo_ready = sem("rh_lo_ready")
        diff_ready = sem("diff_ready")
        change_ready = sem("change_ready")
        h_ready = sem("h_ready")
        h_lo_ready = sem("h_lo_ready")
        nat_lo_ready = sem("nat_lo_ready")
        a_lo_ready = sem("a_lo_ready")
        y_summed = sem("y_summed")
        moments_ready = sem("moments_ready")
        var_ready = sem("var_ready")
        y_ready = sem("y_ready")
        scratch_ready = sem("scratch_ready")
        ident_zero = sem("ident_zero")
        ident_ready = sem("ident_ready")
        exponent_ready = sem("exponent_ready")
        rstd_ready = sem("rstd_ready")

        x_rows = x.rearrange("b (t p) d -> b p t d", p=P)
        out_rows = out.rearrange("b (t p) d -> b p t d", p=P)

        def two_tiles(t, j):
            return t[:, 2 * j:2 * j + 2, :]

        def two_tiles_of(bank):
            return bank[:, :].rearrange("p (t d) -> p t d", t=2)

        block = ctx.enter_context(nc.Block())

        @block.sync
        def _(sp):
            sp.dma_start(x_in[0][:, :, :], x_rows[0]).then_inc(x_loaded[0], 16)
            sp.dma_start(adj_in[:, :, :], adj.rearrange("(t p) m -> p t m", p=P)).then_inc(adj_loaded, 16)
            for w, src in (("w3", w3_w), ("w5", w5_w), ("u5", u5_w)):
                sp.dma_start(w_in[w][:, :, :], src.rearrange("(t p) i -> p t i", p=P)).then_inc(w_loaded[w], 16)
            sp.dma_start(x_in[1][:, :, :], x_rows[1]).then_inc(x_loaded[1], 16)

            def pair(p, last):
                if not last:
                    sp.wait_ge(xt_done, part(p, 1, 1))
                    sp.wait_ge(nat_lo_ready, half(p, 1, 1))
                    sp.wait_ge(x_res_ready, once(p, 1))
                    for s in range(SLOTS):
                        sp.dma_start(x_in[s][:, :, :], x_rows[SLOTS * p + (SLOTS + s)]).then_inc(x_loaded[s], 16)
                for s in range(SLOTS):
                    sp.wait_ge(y_ready, once(p, s))
                    sp.dma_start(out_rows[SLOTS * p + s], y[s][:, :, :]).then_inc(y_stored[s], 16)

            with sp.Fori(0, PAIRS - 1) as p:
                pair(p, False)
            pair(PAIRS - 1, True)
            for s in range(SLOTS):
                sp.wait_ge(y_stored[s], stored(PAIRS))

        @block.gpsimd
        def _(pool):
            nc.gpsimd.memset(table_scratch[:, :], 0.0).then_inc(scratch_ready, 1)
            pool.sem_inc(y_summed, SLOTS * HALVES)
            for s in range(SLOTS):
                pool.sem_inc(y_stored[s], 16)
            nc.gpsimd.memset(ident[:, :], 0.0).then_inc(ident_zero, 1)
            pool.wait_ge(ident_zero, 1)
            nc.gpsimd.affine_select(out=ident[:, :], in_=ident[:, :], compare_op=ALU.not_equal, fill=1.0, base=0,
                                    pattern=[[-1, P]], channel_multiplier=1).then_inc(ident_ready, 1)
            for i, src in enumerate((w3_b, w4_b, w5_b, u3_b, u5_b)):
                pool.dma_start(bias_in[:, i, :], src.rearrange("(t p) -> p t", p=P),
                               allow_slow_non_contiguous=True).then_inc(bias_loaded, 16)
            nc.gpsimd.memset(minus_half[:, :], -0.5).then_inc(exponent_ready, 1)
            pool.wait_ge(exponent_ready, 1)

            def pair(p):
                for s in range(SLOTS):
                    pool.wait_ge(var_ready, once(p, s))
                    nc.gpsimd.tensor_tensor(rstd[s][:, :], var_eps[s][:, :], minus_half[:, :],
                                            ALU.pow).then_inc(rstd_ready, 1)

            with pool.Fori(0, PAIRS) as p:
                pair(p)

        @block.tensor
        def _(pe):
            def product(bank, w_hi, w_lo, m_hi, m_lo, first, last):
                nc.tensor.matmul(bank[:, :], w_hi, m_hi, start=first, stop=False)
                nc.tensor.matmul(bank[:, :], w_hi, m_lo, start=False, stop=False)
                return nc.tensor.matmul(bank[:, :], w_lo, m_hi, start=False, stop=last)

            def weigh(bank, w, j, m_hi, m_lo, first=True, last=True):
                for d in range(DT):
                    cols = slice(j * P, (j + 1) * P)
                    done = product(bank, wT_hi[w][:, d, cols], wT_lo[w][:, d, cols], m_hi[:, d, :], m_lo[:, d, :],
                                   first and d == 0, last and d == DT - 1)
                return done

            def adjacency(p, k, j, t0=0, t1=NT, first=False):
                s = k % SLOTS
                if t0 == 0 and not first:
                    pe.wait_ge(r_ready, half(p, k - 1, j))
                for t in range(t0, t1):
                    if j == 0 and t % 2 == 0:
                        pe.wait_ge(nat_lo_ready, half(p, k, t // 2))
                    if j == 0 and first:
                        pe.wait_ge(prep_lo, t + 1)
                    cols = slice(j * P, (j + 1) * P)
                    done = product(ra_bank[j], nat_hi[s][:, t, cols], nat_lo[s][:, t, cols],
                                   adjT_hi[:, t, :], adjT_lo[:, t, :], t == 0, t == NT - 1)
                if t1 == NT:
                    done.then_inc(a_done, 1)

            def transpose_x(s, j):
                for t in range(NT):
                    done = nc.tensor.transpose(ut_bank[j][:, t * P:(t + 1) * P], x_in[s][:, t, j * P:(j + 1) * P],
                                               ident[:, :])
                done.then_inc(xt_done, 1)

            def transpose_h(s, j):
                for i in range(2):
                    for d in range(DT):
                        done = nc.tensor.transpose(ut_bank[j][:, (i * DT + d) * P:(i * DT + d + 1) * P],
                                                   hT[s][:, d, (2 * j + i) * P:(2 * j + i + 1) * P], ident[:, :])
                done.then_inc(t_done, 1)

            def prepare(q):
                what, i, bank = PREP[q]
                if what == "adj":
                    tiles = [adj_in[:, t, i * P:(i + 1) * P] for t in range(NT)]
                else:
                    tiles = [w_nat[what][:, t, d * P:(d + 1) * P] for d in range(DT) for t in range(DT)]
                for n, tile in enumerate(tiles):
                    done = nc.tensor.transpose(banks[bank][:, n * P:(n + 1) * P], tile, ident[:, :])
                done.then_inc(prep_done, 1)

            pe.wait_ge(ident_ready, 1)
            pe.wait_ge(x_loaded[0], 16)
            for j in range(HALVES):
                transpose_x(0, j)
            pe.wait_ge(adj_loaded, 16)
            for q in range(4):
                prepare(q)
            adjacency(0, 0, 0, first=True)
            for q in range(4, len(PREP)):
                if PREP[q][0] in w_sum:
                    pe.wait_ge(w_added, 1 + list(w_sum).index(PREP[q][0]))
                else:
                    pe.wait_ge(w_loaded[PREP[q][0]], 16)
                if q == len(PREP) - 1:
                    pe.wait_ge(xt_copied, part(0, 0, 0))
                prepare(q)
            adjacency(0, 0, 1, first=True)
            pe.wait_ge(xt_copied, part(0, 0, 1))
            pe.wait_ge(prep_lo, len(PREP))

            def pair(p, last):
                for k in range(UNITS):
                    s = k % SLOTS
                    pe.wait_ge(h_lo_ready, half(p, k, 1))
                    for j in range(HALVES):
                        if k == 0:
                            pe.wait_ge(y_summed, summed(p - 1, 1, 1))
                        elif k == 1:
                            pe.wait_ge(xt_copied, part(p, 1, j))
                        else:
                            pe.wait_ge(nat_lo_ready, half(p, k, j))
                        weigh(ut_bank[j], "u3", j, hT_hi[s], hT_lo[s]).then_inc(u_done, 1)
                    pe.wait_ge(a_lo_ready, half(p, k, 1))
                    for j in range(HALVES):
                        weigh(ra_bank[j], "w4", j, aT_hi, aT_lo).then_inc(r_done, 1)
                    if k > 0:
                        pe.wait_ge(h_ready, half(p, k - 1, 1))
                        for j in range(HALVES):
                            pe.wait_ge(u_copied, half(p, k, j))
                            transpose_h(1 - s, j)
                    if k > 0:
                        pe.wait_ge(z_ready, half(p, k - 1, 1))
                    for j in range(HALVES):
                        weigh(z_bank[j], "w3", j, aT_hi, aT_lo).then_inc(z_done, 1)
                    if k == 0:
                        pe.wait_ge(x_loaded[1], 16 * p + 16)
                        for j in range(HALVES):
                            pe.wait_ge(u_copied, half(p, 0, j))
                            transpose_x(1, j)
                    if k > 0:
                        pe.wait_ge(v_ready, half(p, k - 1, 1))
                    for j in range(HALVES):
                        weigh(v_bank[j], "w5", j, aT_hi, aT_lo, last=False)
                    if k < UNITS - 1:
                        for j in range(HALVES):
                            adjacency(p, k + 1, j)
                    elif not last:
                        pe.wait_ge(x_loaded[0], 16 * p + 32)
                        for j in range(HALVES):
                            pe.wait_ge(y_summed, summed(p, 0, j))
                            transpose_x(0, j)
                    pe.wait_ge(rh_lo_ready, half(p, k, 1))
                    for j in range(HALVES):
                        weigh(v_bank[j], "u5", j, rh_hi, rh_lo, first=False).then_inc(v_done, 1)
                if not last:
                    adjacency(p, UNITS, 0)
                    adjacency(p, UNITS, 1, 0, NT // 2)
                pe.wait_ge(h_ready, half(p, UNITS - 1, 1))
                for j in range(HALVES):
                    if last:
                        pe.wait_ge(y_summed, summed(p, 0, j))
                    else:
                        pe.wait_ge(xt_copied, part(p, SLOTS, j))
                    transpose_h(1, j)
                if not last:
                    adjacency(p, UNITS, 1, NT // 2, NT)

            with pe.Fori(0, PAIRS - 1) as p:
                pair(p, False)
            pair(PAIRS - 1, True)

        @block.scalar
        def _(act):
            for w, src in (("u3", u3_w), ("w4", w4_w)):
                act.dma_start(w_in[w][:, :, :], src.rearrange("(t p) i -> p t i", p=P)).then_inc(w_loaded[w], 16)

            def state_hi(p, k, s, j):
                nc.scalar.copy(hT_hi[s][:, j, :], hT[s][:, j, :]).then_inc(h_hi_ready, 1)

            def new_state(p, s):
                for j in range(HALVES):
                    act.wait_ge(xt_done, part(p, s, j))
                    nc.scalar.copy(hT[s][:, j, :], ut_bank[j][:, :]).then_inc(xt_copied, 1)

            def new_state_hi(p, s):
                for j in range(HALVES):
                    act.wait_ge(xt_copied, part(p, s, j))
                    state_hi(p, s, s, j)

            def new_rows(p, s):
                act.wait_ge(x_loaded[s], 16 * p + 16)
                for j in range(HALVES):
                    nc.scalar.copy(two_tiles(nat_hi[s], j), two_tiles(x_in[s], j)).then_inc(nat_hi_ready, 1)

            def keep_x(p, s):
                act.wait_ge(y_summed, summed(p - 1, s, 1))
                nc.scalar.copy(x_res[s][:, :, :], x_in[s][:, :, :]).then_inc(x_res_ready, 1)

            def a_high(p, k, j):
                act.wait_ge(a_done, half(p, k, j))
                nc.scalar.copy(aT_hi[:, j, :], ra_bank[j][:, :]).then_inc(a_hi_ready, 1)

            def load_table():
                nc.scalar.activation(table_scratch[:, :], table_scratch[:, :], ACT.Sigmoid)

            act.wait_ge(scratch_ready, 1)
            load_table()
            new_rows(0, 0)
            for q, (what, i, bank) in enumerate(PREP):
                if q == 4:
                    new_state(0, 0)
                    new_state_hi(0, 0)
                    a_high(0, 0, 0)
                act.wait_ge(prep_done, q + 1)
                dst = adjT_hi[:, i, :] if what == "adj" else wT_hi[what].rearrange("p t d -> p (t d)")
                nc.scalar.copy(dst, banks[bank][:, :]).then_inc(prep_hi, 1)
            a_high(0, 0, 1)
            keep_x(0, 0)
            act.wait_ge(bias_ready, 3)
            act.wait_ge(prep_lo, len(PREP))

            def pair(p, last):
                def candidate(k):
                    for j in range(HALVES):
                        act.wait_ge(v_done, half(p, k, j))
                        nc.scalar.activation(v_sb[:, j, :], v_bank[j][:, :], ACT.Tanh,
                                             bias=bias[:, 2, j:j + 1]).then_inc(v_ready, 1)

                for k in range(UNITS):
                    s = k % SLOTS
                    for j in range(HALVES):
                        act.wait_ge(u_done, half(p, k, j))
                        nc.scalar.copy(u_sb[:, j, :], ut_bank[j][:, :]).then_inc(u_copied, 1)
                    if 0 < k <= LAST_STEP:
                        for j in range(HALVES):
                            act.wait_ge(h_ready, half(p, k - 1, j))
                            state_hi(p, k + 1, 1 - s, j)
                    if k == 0:
                        new_rows(p, 1)
                    for j in range(HALVES):
                        act.wait_ge(r_summed, half(p, k, j))
                        nc.scalar.activation(r_sb[:, j, :], ra_bank[j][:, :], ACT.Sigmoid,
                                             bias=bias[:, 1, j:j + 1]).then_inc(r_ready, 1)
                    if 0 < k <= LAST_STEP:
                        for j in range(HALVES):
                            act.wait_ge(t_done, half(p, k - 1, j))
                            nc.scalar.copy(two_tiles(nat_hi[1 - s], j),
                                           two_tiles_of(ut_bank[j])).then_inc(nat_hi_ready, 1)
                    for j in range(HALVES):
                        act.wait_ge(rh_ready, half(p, k, j))
                        nc.scalar.copy(rh_hi[:, j, :], rh[:, j, :]).then_inc(rh_hi_ready, 1)
                    if k == UNITS - 1 and not last:
                        new_rows(p + 1, 0)
                    for j in range(HALVES):
                        act.wait_ge(z_summed, half(p, k, j))
                        nc.scalar.activation(z_sb[:, j, :], z_bank[j][:, :], ACT.Sigmoid,
                                             bias=bias[:, 0, j:j + 1]).then_inc(z_ready, 1)
                    if k == 0:
                        new_state(p, 1)
                        new_state_hi(p, 1)
                        keep_x(p, 1)
                    if k < UNITS - 1:
                        for j in range(HALVES):
                            a_high(p, k + 1, j)
                        candidate(k)
                    else:
                        if not last:
                            new_state(p + 1, 0)
                        candidate(k)
                        if not last:
                            new_state_hi(p + 1, 0)
                            for j in range(HALVES):
                                a_high(p, UNITS, j)
                            keep_x(p + 1, 0)

            with act.Fori(0, PAIRS - 1) as p:
                load_table()
                pair(p, False)
            pair(PAIRS - 1, True)

        @block.vector
        def _(dve):
            def new_rows_low(p, s):
                for j in range(HALVES):
                    dve.wait_ge(nat_hi_ready, half(p, s, j))
                    nc.vector.tensor_tensor(two_tiles(nat_lo[s], j), two_tiles(x_in[s], j), two_tiles(nat_hi[s], j),
                                            ALU.subtract).then_inc(nat_lo_ready, 1)

            def state_low(p, k, s):
                for j in range(HALVES):
                    dve.wait_ge(h_hi_ready, half(p, k, j))
                    nc.vector.tensor_tensor(hT_lo[s][:, j, :], hT[s][:, j, :], hT_hi[s][:, j, :],
                                            ALU.subtract).then_inc(h_lo_ready, 1)

            def a_low(p, k, j):
                dve.wait_ge(a_hi_ready, half(p, k, j))
                nc.vector.tensor_tensor(aT_lo[:, j, :], ra_bank[j][:, :], aT_hi[:, j, :],
                                        ALU.subtract).then_inc(a_lo_ready, 1)

            def prepare_low(q):
                what, i, bank = PREP[q]
                hi, lo = (adjT_hi[:, i, :], adjT_lo[:, i, :]) if what == "adj" else \
                    (wT_hi[what].rearrange("p t d -> p (t d)"), wT_lo[what].rearrange("p t d -> p (t d)"))
                dve.wait_ge(prep_hi, q + 1)
                nc.vector.tensor_tensor(lo, banks[bank][:, :], hi, ALU.subtract).then_inc(prep_lo, 1)

            new_rows_low(0, 0)
            for q in range(4):
                prepare_low(q)
            for w, total in w_sum.items():
                dve.wait_ge(w_loaded[w], 16)
                nc.vector.tensor_tensor(total, w_in[w][:, :, 0:D], w_in[w][:, :, D:2 * D],
                                        ALU.add).then_inc(w_added, 1)
            state_low(0, 0, 0)
            dve.wait_ge(bias_loaded, 16 * len(BIASES))
            for i, (a, b) in enumerate((("w3", "u3"), ("w4", "u3"), ("w5", "u5"))):
                nc.vector.tensor_tensor(bias[:, i, :], bias_in[:, BIASES.index(a), :],
                                        bias_in[:, BIASES.index(b), :], ALU.add).then_inc(bias_ready, 1)
            a_low(0, 0, 0)
            for q in range(4, len(PREP)):
                prepare_low(q)
            a_low(0, 0, 1)

            def pair(p, last):
                def update(k):
                    s = k % SLOTS

                    def diff(j):
                        dve.wait_ge(v_ready, half(p, k, j))
                        nc.vector.tensor_tensor(change[:, j, :], v_sb[:, j, :], hT[s][:, j, :],
                                                ALU.subtract).then_inc(diff_ready, 1)

                    def gate(j):
                        dve.wait_ge(diff_ready, half(p, k, j))
                        dve.wait_ge(z_ready, half(p, k, j))
                        nc.vector.tensor_tensor(change[:, j, :], z_sb[:, j, :], change[:, j, :],
                                                ALU.mult).then_inc(change_ready, 1)

                    def add(j):
                        dve.wait_ge(change_ready, half(p, k, j))
                        nc.vector.tensor_tensor(hT[s][:, j, :], hT[s][:, j, :], change[:, j, :],
                                                ALU.add).then_inc(h_ready, 1)

                    diff(0)
                    gate(0)
                    diff(1)
                    add(0)
                    gate(1)
                    add(1)

                def residual(s):
                    dve.wait_ge(y_stored[s], stored(p))
                    dve.wait_ge(x_res_ready, once(p, s))
                    for j in range(HALVES):
                        dve.wait_ge(t_done, half(p, LAST_STEP + s, j))
                        nc.vector.tensor_tensor(two_tiles(y[s], j), two_tiles_of(ut_bank[j]), two_tiles(x_res[s], j),
                                                ALU.add).then_inc(y_summed, 1)

                def statistics(s):
                    for t in range(NT):
                        if t % 2 == 0:
                            dve.wait_ge(y_summed, summed(p, s, t // 2))
                        nc.vector.bn_stats(stats[s][:, t, :], y[s][:, t, :])
                    dve.drain()
                    for t in range(NT):
                        done = nc.vector.bn_aggr(moments[s][:, t, :], stats[s][:, t, :])
                    done.then_inc(moments_ready, 1)
                    dve.wait_ge(moments_ready, once(p, s))
                    nc.vector.tensor_scalar(var_eps[s][:, :], moments[s][:, :, 1], EPS, None,
                                            ALU.add).then_inc(var_ready, 1)

                def normalise(s):
                    dve.wait_ge(rstd_ready, once(p, s))
                    for t in range(NT):
                        done = nc.vector.tensor_scalar(y[s][:, t, :], y[s][:, t, :], moments[s][:, t, 0:1],
                                                       rstd[s][:, t:t + 1], ALU.subtract, ALU.mult)
                    done.then_inc(y_ready, 1)

                for k in range(UNITS):
                    s = k % SLOTS
                    if k > 0:
                        update(k - 1)
                    else:
                        new_rows_low(p, 1)
                    for j in range(HALVES):
                        dve.wait_ge(r_done, half(p, k, j))
                        dve.wait_ge(u_copied, half(p, k, j))
                        nc.vector.tensor_tensor(ra_bank[j][:, :], ra_bank[j][:, :], u_sb[:, j, :],
                                                ALU.add).then_inc(r_summed, 1)
                    for j in range(HALVES):
                        dve.wait_ge(r_ready, half(p, k, j))
                        nc.vector.tensor_tensor(rh[:, j, :], r_sb[:, j, :], hT[s][:, j, :],
                                                ALU.mult).then_inc(rh_ready, 1)
                    if 0 < k <= LAST_STEP:
                        for j in range(HALVES):
                            dve.wait_ge(nat_hi_ready, half(p, k + 1, j))
                            nc.vector.tensor_tensor(two_tiles(nat_lo[1 - s], j), two_tiles_of(ut_bank[j]),
                                                    two_tiles(nat_hi[1 - s], j),
                                                    ALU.subtract).then_inc(nat_lo_ready, 1)
                    for j in range(HALVES):
                        dve.wait_ge(rh_hi_ready, half(p, k, j))
                        nc.vector.tensor_tensor(rh_lo[:, j, :], rh[:, j, :], rh_hi[:, j, :],
                                                ALU.subtract).then_inc(rh_lo_ready, 1)
                    if 0 < k <= LAST_STEP:
                        state_low(p, k + 1, 1 - s)
                    if k == UNITS - 1:
                        residual(0)
                    for j in range(HALVES):
                        dve.wait_ge(z_done, half(p, k, j))
                        nc.vector.tensor_tensor(z_bank[j][:, :], z_bank[j][:, :], u_sb[:, j, :],
                                                ALU.add).then_inc(z_summed, 1)
                    if k == 0:
                        state_low(p, 1, 1)
                    if k < UNITS - 1:
                        for j in range(HALVES):
                            a_low(p, k + 1, j)
                statistics(0)
                if not last:
                    new_rows_low(p + 1, 0)
                update(UNITS - 1)
                if not last:
                    a_low(p, UNITS, 0)
                    state_low(p, UNITS, 0)
                residual(1)
                if not last:
                    a_low(p, UNITS, 1)
                normalise(0)
                statistics(1)
                normalise(1)

            with dve.Fori(0, PAIRS - 1) as p:
                pair(p, False)
            pair(PAIRS - 1, True)


_INS = ['x', 'adj', 'L0_gnn_w3_w', 'L0_gnn_w3_b', 'L0_gnn_u3_w', 'L0_gnn_u3_b', 'L0_gnn_w4_w', 'L0_gnn_w4_b',
        'L0_gnn_w5_w', 'L0_gnn_w5_b', 'L0_gnn_u5_w', 'L0_gnn_u5_b']
_OUTS = [((16, 512, 256), 'float32')]


def kernel(**inputs):
    import numpy as _np
    import concourse.bacc as _bacc
    from concourse import mybir as _mybir
    from concourse.bass_utils import run_bass_kernel_spmd as _run

    nc = _bacc.Bacc("TRN2", target_bir_lowering=False, num_devices=1)
    arrays, args = {}, []
    for name in _INS:
        a = _np.ascontiguousarray(inputs[name])
        arrays[f"in_{name}_dram"] = a
        args.append(nc.dram_tensor(f"in_{name}_dram", a.shape, _mybir.dt.from_np(a.dtype), kind="ExternalInput").ap())
    for i, (shape, dtype) in enumerate(_OUTS):
        dt = _mybir.dt.from_np(_np.dtype(dtype))
        args.append(nc.dram_tensor(f"out_{i}_dram", shape, dt, kind="ExternalOutput").ap())
    gated_graph_steps_kernel(nc, *args)
    r = _run(nc, [arrays], core_ids=[0])
    return r.results[0]["out_0_dram"]
```

```python
from contextlib import ExitStack

import concourse.bass as bass
from concourse import mybir


def gated_graph_steps_kernel(nc: bass.Bass, x, adj, w3_w, w3_b, u3_w, u3_b, w4_w, w4_b,
                             w5_w, w5_b, u5_w, u5_b, out):
    F32 = mybir.dt.float32
    F32R = mybir.dt.float32r
    ALU = mybir.AluOpType
    ACT = mybir.ActivationFunctionType

    P = 128
    B, N, D = x.shape
    STEPS = 3
    SLOTS = 2
    PAIRS = B // SLOTS
    UNITS = STEPS * SLOTS
    NT = N // P
    DT = D // P
    HALVES = 2
    EPS = 1e-5
    LAST_STEP = UNITS - SLOTS
    QUAD = 32
    QUADS = P // QUAD
    MOVES = QUADS
    assert NT == QUADS and DT == HALVES and N == 512 and PAIRS >= 3

    def half(p, k, j):
        return 2 * UNITS * p + (2 * k + j + 1)

    def part(p, s, j):
        return 2 * SLOTS * p + (2 * s + j + 1)

    def once(p, s):
        return SLOTS * p + (s + 1)

    def summed(p, s, t):
        return SLOTS * NT * p + (NT * s + t + 1)

    def stored(p):
        return 16 * (p + 1)

    def moved(p, k):
        return 16 * MOVES * STEPS * p + 16 * MOVES * (k // SLOTS + 1)

    def x_moved(p):
        return 16 * MOVES * (p + 1)

    ctx = ExitStack()
    with ctx:
        def sb(name, shape, dt=F32):
            return ctx.enter_context(nc.sbuf_tensor(name, shape, dt))

        def sem(name):
            return ctx.enter_context(nc.semaphore(name))

        adjT_hi = sb("adjT_hi", [P, NT, N], F32R)
        adjT_lo = sb("adjT_lo", [P, NT, N], F32R)
        WEIGHTS = ("u3", "w4", "w3", "w5", "u5")
        wT_hi = {w: sb(f"{w}T_hi", [P, DT, D], F32R) for w in WEIGHTS}
        wT_lo = {w: sb(f"{w}T_lo", [P, DT, D], F32R) for w in WEIGHTS}
        BIASES = ("w3", "w4", "w5", "u3", "u5")
        bias_in = sb("bias_in", [P, len(BIASES), DT])
        bias = sb("bias", [P, 3, DT])
        ident = sb("ident", [P, P])
        minus_half = sb("minus_half", [P, NT])
        table_scratch = sb("table_scratch", [P, 1])

        x_in = [sb(f"x_in{s}", [P, NT, D]) for s in range(SLOTS)]
        x_mixed = [sb(f"x_mixed{s}", [P, NT, D]) for s in range(SLOTS)]
        x_res = [sb(f"x_res{s}", [P, NT, D]) for s in range(SLOTS)]
        x_blocks = [sb(f"x_blocks{s}", [P, NT * D]) for s in range(SLOTS)]
        h_blocks = [sb(f"h_blocks{s}", [P, NT * D]) for s in range(SLOTS)]
        nat = [sb(f"nat{s}", [P, NT * D]) for s in range(SLOTS)]
        nat_hi = [sb(f"nat_hi{s}", [P, NT * D], F32R) for s in range(SLOTS)]
        nat_lo = [sb(f"nat_lo{s}", [P, NT * D], F32R) for s in range(SLOTS)]
        hT = [sb(f"hT{s}", [P, DT, N]) for s in range(SLOTS)]
        hT_hi = [sb(f"hT_hi{s}", [P, DT, N], F32R) for s in range(SLOTS)]
        hT_lo = [sb(f"hT_lo{s}", [P, DT, N], F32R) for s in range(SLOTS)]
        y = [sb(f"y{s}", [P, NT, D]) for s in range(SLOTS)]
        stats = [sb(f"stats{s}", [P, NT, 6]) for s in range(SLOTS)]
        moments = [sb(f"moments{s}", [P, NT, 2]) for s in range(SLOTS)]
        var_eps = [sb(f"var_eps{s}", [P, NT]) for s in range(SLOTS)]
        rstd = [sb(f"rstd{s}", [P, NT]) for s in range(SLOTS)]

        aT_hi = sb("aT_hi", [P, DT, N], F32R)
        aT_lo = sb("aT_lo", [P, DT, N], F32R)
        u_sb = sb("u_sb", [P, DT, N])
        r_sb = sb("r_sb", [P, DT, N])
        z_sb = sb("z_sb", [P, DT, N])
        v_sb = sb("v_sb", [P, DT, N])
        rh = sb("rh", [P, DT, N])
        rh_hi = sb("rh_hi", [P, DT, N], F32R)
        rh_lo = sb("rh_lo", [P, DT, N], F32R)
        change = sb("change", [P, DT, N])

        adj_in = sb("adj_in", [P, NT, N])
        w_in = {"w3": v_sb, "w4": r_sb, "w5": z_sb,
                "u3": change[:, 0, :].rearrange("p (t d) -> p t d", t=DT),
                "u5": change[:, 1, :].rearrange("p (t d) -> p t d", t=DT)}
        w_sum = {"w4": rh[:, 0, :].rearrange("p (t d) -> p t d", t=DT),
                 "w3": rh[:, 1, :].rearrange("p (t d) -> p t d", t=DT),
                 "w5": u_sb[:, 0, :].rearrange("p (t d) -> p t d", t=DT)}
        w_nat = {**w_sum, "u3": w_in["u3"], "u5": w_in["u5"]}

        banks = [ctx.enter_context(nc.psum_tensor(f"bank{i}", [P, N], F32)) for i in range(8)]
        u_bank, ra_bank, z_bank, v_bank = banks[0:2], banks[2:4], banks[4:6], banks[6:8]
        PREP = [("adj", 0, 4), ("adj", 1, 5), ("adj", 2, 6), ("adj", 3, 7),
                ("u3", 0, 4), ("w4", 0, 5), ("w3", 0, 6), ("w5", 0, 7), ("u5", 0, 0)]

        x_loaded = [sem(f"x_loaded{s}") for s in range(SLOTS)]
        x_mixed_loaded = [sem(f"x_mixed_loaded{s}") for s in range(SLOTS)]
        x_kept = [sem(f"x_kept{s}") for s in range(SLOTS)]
        hT_moved = [sem(f"hT_moved{s}") for s in range(SLOTS)]
        nat_moved = [sem(f"nat_moved{s}") for s in range(SLOTS)]
        y_stored = [sem(f"y_stored{s}") for s in range(SLOTS)]
        adj_loaded = sem("adj_loaded")
        w_loaded = {w: sem(f"{w}_loaded") for w in WEIGHTS}
        bias_loaded = sem("bias_loaded")
        prep_done = sem("prep_done")
        u_done = sem("u_done")
        r_done = sem("r_done")
        z_done = sem("z_done")
        v_done = sem("v_done")
        a_done = sem("a_done")
        prep_hi = sem("prep_hi")
        u_copied = sem("u_copied")
        r_ready = sem("r_ready")
        z_ready = sem("z_ready")
        v_ready = sem("v_ready")
        rh_hi_ready = sem("rh_hi_ready")
        h_hi_ready = sem("h_hi_ready")
        nat_hi_ready = sem("nat_hi_ready")
        a_hi_ready = sem("a_hi_ready")
        w_added = sem("w_added")
        prep_lo = sem("prep_lo")
        bias_ready = sem("bias_ready")
        r_summed = sem("r_summed")
        z_summed = sem("z_summed")
        rh_ready = sem("rh_ready")
        rh_lo_ready = sem("rh_lo_ready")
        diff_ready = sem("diff_ready")
        change_ready = sem("change_ready")
        h_ready = sem("h_ready")
        h_blocks_ready = sem("h_blocks_ready")
        x_blocks_ready = sem("x_blocks_ready")
        h_lo_ready = sem("h_lo_ready")
        nat_lo_ready = sem("nat_lo_ready")
        a_lo_ready = sem("a_lo_ready")
        y_summed = sem("y_summed")
        moments_ready = sem("moments_ready")
        var_ready = sem("var_ready")
        y_ready = sem("y_ready")
        scratch_ready = sem("scratch_ready")
        ident_zero = sem("ident_zero")
        ident_ready = sem("ident_ready")
        exponent_ready = sem("exponent_ready")
        rstd_ready = sem("rstd_ready")

        x_rows = x.rearrange("b (t p) d -> b p t d", p=P)
        x_mixed_rows = x.rearrange("b (p t) d -> b p t d", p=P)
        out_rows = out.rearrange("b (t p) d -> b p t d", p=P)

        HALF = NT * D // HALVES

        def flat_half(t, j):
            return t[:, j * HALF:(j + 1) * HALF]

        def by_quads(t, j):
            return t[:, :].rearrange("p (c a i) -> p a c i", a=QUADS, i=QUAD)[:, 2 * j:2 * j + 2]

        def nat_half(t, j):
            return t[:, :].rearrange("p (a c i) -> p a c i", a=QUADS, i=QUAD)[:, 2 * j:2 * j + 2]

        def flat(t):
            return t[:, :, :].rearrange("p t d -> p (t d)")

        block = ctx.enter_context(nc.Block())

        @block.sync
        def _(sp):
            def move_h(p, k):
                s = k % SLOTS
                sp.wait_ge(h_blocks_ready, half(p, k, 1))
                for a in range(QUADS):
                    sp.dma_start(nat[s][:, a * D:(a + 1) * D],
                                 h_blocks[s][a * QUAD:(a + 1) * QUAD, :].rearrange("j (b x) -> j b x", b=QUADS)
                                 ).then_inc(nat_moved[s], 16)

            def move_x(p, s):
                sp.wait_ge(x_blocks_ready, part(p, s, 1))
                for q in range(QUADS):
                    sp.dma_start(hT[s][:, :, q * P:(q + 1) * P],
                                 x_blocks[s][q * QUAD:(q + 1) * QUAD, :].rearrange("i (a d n) -> i a d n",
                                                                                  a=QUADS, d=DT)
                                 ).then_inc(hT_moved[s], 16)

            sp.dma_start(adj_in[:, :, :], adj.rearrange("(t p) m -> p t m", p=P)).then_inc(adj_loaded, 16)
            sp.dma_start(x_in[0][:, :, :], x_rows[0]).then_inc(x_loaded[0], 16)
            sp.dma_start(x_mixed[0][:, :, :], x_mixed_rows[0]).then_inc(x_mixed_loaded[0], 16)
            move_x(0, 0)
            sp.dma_start(x_mixed[1][:, :, :], x_mixed_rows[1]).then_inc(x_mixed_loaded[1], 16)
            sp.dma_start(x_in[1][:, :, :], x_rows[1]).then_inc(x_loaded[1], 16)
            move_x(0, 1)

            def store(p, s):
                sp.wait_ge(y_ready, once(p, s))
                sp.dma_start(out_rows[SLOTS * p + s], y[s][:, :, :]).then_inc(y_stored[s], 16)

            def pair(p, first, last):
                for k in range(UNITS):
                    move_h(p, k)
                    if k == 0:
                        if not first:
                            store(p - 1, 1)
                        for s in range(SLOTS):
                            sp.wait_ge(x_loaded[s], 16 * p + 16)
                            sp.dma_start(x_res[s][:, :, :], x_in[s][:, :, :]).then_inc(x_kept[s], 16)
                    if k >= LAST_STEP and not last:
                        move_x(p + 1, k % SLOTS)
                    if k < LAST_STEP and not last:
                        if k == 0:
                            sp.wait_ge(nat_lo_ready, half(p, 1, 1))
                            sp.wait_ge(x_blocks_ready, part(p, 1, 1))
                            for s in range(SLOTS):
                                sp.wait_ge(x_kept[s], 16 * p + 16)
                        s = k % SLOTS
                        row = SLOTS * p + (SLOTS + s)
                        if k < SLOTS:
                            sp.dma_start(x_mixed[s][:, :, :], x_mixed_rows[row]).then_inc(x_mixed_loaded[s], 16)
                        else:
                            sp.dma_start(x_in[s][:, :, :], x_rows[row]).then_inc(x_loaded[s], 16)
                store(p, 0)

            pair(0, True, False)
            with sp.Fori(1, PAIRS - 1) as p:
                pair(p, False, False)
            pair(PAIRS - 1, False, True)
            store(PAIRS - 1, 1)
            for s in range(SLOTS):
                sp.wait_ge(y_stored[s], stored(PAIRS))

        @block.gpsimd
        def _(pool):
            nc.gpsimd.memset(table_scratch[:, :], 0.0).then_inc(scratch_ready, 1)
            for s in range(SLOTS):
                pool.sem_inc(y_stored[s], 16)
            nc.gpsimd.memset(ident[:, :], 0.0).then_inc(ident_zero, 1)
            pool.wait_ge(ident_zero, 1)
            nc.gpsimd.affine_select(out=ident[:, :], in_=ident[:, :], compare_op=ALU.not_equal, fill=1.0, base=0,
                                    pattern=[[-1, P]], channel_multiplier=1).then_inc(ident_ready, 1)
            pool.wait_ge(x_loaded[0], 16)
            for w, src in (("u3", u3_w), ("w4", w4_w), ("w3", w3_w), ("w5", w5_w), ("u5", u5_w)):
                pool.dma_start(w_in[w][:, :, :], src.rearrange("(t p) i -> p t i", p=P)).then_inc(w_loaded[w], 16)
            for i, src in enumerate((w3_b, w4_b, w5_b, u3_b, u5_b)):
                pool.dma_start(bias_in[:, i, :], src.rearrange("(t p) -> p t", p=P),
                               allow_slow_non_contiguous=True).then_inc(bias_loaded, 16)
            nc.gpsimd.memset(minus_half[:, :], -0.5).then_inc(exponent_ready, 1)
            pool.wait_ge(exponent_ready, 1)

            def pair(p):
                for s in range(SLOTS):
                    pool.wait_ge(var_ready, once(p, s))
                    nc.gpsimd.tensor_tensor(rstd[s][:, :], var_eps[s][:, :], minus_half[:, :],
                                            ALU.pow).then_inc(rstd_ready, 1)

            with pool.Fori(0, PAIRS) as p:
                pair(p)

        @block.tensor
        def _(pe):
            def product(bank, w_hi, w_lo, m_hi, m_lo, first, last):
                nc.tensor.matmul(bank[:, :], w_hi, m_hi, start=first, stop=False)
                nc.tensor.matmul(bank[:, :], w_hi, m_lo, start=False, stop=False)
                return nc.tensor.matmul(bank[:, :], w_lo, m_hi, start=False, stop=last)

            def weigh(bank, w, j, m_hi, m_lo, first=True, last=True):
                for d in range(DT):
                    cols = slice(j * P, (j + 1) * P)
                    done = product(bank, wT_hi[w][:, d, cols], wT_lo[w][:, d, cols], m_hi[:, d, :], m_lo[:, d, :],
                                   first and d == 0, last and d == DT - 1)
                return done

            def adjacency(p, k, j, first=False):
                s = k % SLOTS
                if not first:
                    pe.wait_ge(r_ready, half(p, k - 1, j))
                for t in range(NT):
                    if j == 0 and t == 0:
                        pe.wait_ge(nat_lo_ready, half(p, k, 1))
                    if j == 0 and first:
                        pe.wait_ge(prep_lo, t + 1)
                    hi, lo = (n[s][:, t * D + j * P:t * D + (j + 1) * P] for n in (nat_hi, nat_lo))
                    done = product(ra_bank[j], hi, lo, adjT_hi[:, t, :], adjT_lo[:, t, :], t == 0, t == NT - 1)
                done.then_inc(a_done, 1)

            def prepare(q):
                what, i, bank = PREP[q]
                if what == "adj":
                    tiles = [adj_in[:, t, i * P:(i + 1) * P] for t in range(NT)]
                else:
                    tiles = [w_nat[what][:, t, d * P:(d + 1) * P] for d in range(DT) for t in range(DT)]
                for n, tile in enumerate(tiles):
                    done = nc.tensor.transpose(banks[bank][:, n * P:(n + 1) * P], tile, ident[:, :])
                done.then_inc(prep_done, 1)

            pe.wait_ge(ident_ready, 1)
            pe.wait_ge(adj_loaded, 16)
            for q in range(4):
                prepare(q)
            adjacency(0, 0, 0, first=True)
            for q in range(4, len(PREP)):
                if PREP[q][0] in w_sum:
                    pe.wait_ge(w_added, 1 + list(w_sum).index(PREP[q][0]))
                else:
                    pe.wait_ge(w_loaded[PREP[q][0]], 16)
                prepare(q)
            adjacency(0, 0, 1, first=True)
            pe.wait_ge(prep_lo, len(PREP))

            def pair(p, last):
                for k in range(UNITS):
                    s = k % SLOTS
                    pe.wait_ge(h_lo_ready, half(p, k, 1))
                    for j in range(HALVES):
                        weigh(u_bank[j], "u3", j, hT_hi[s], hT_lo[s]).then_inc(u_done, 1)
                    pe.wait_ge(a_lo_ready, half(p, k, 1))
                    for j in range(HALVES):
                        weigh(ra_bank[j], "w4", j, aT_hi, aT_lo).then_inc(r_done, 1)
                    if k > 0:
                        pe.wait_ge(z_ready, half(p, k - 1, 1))
                    for j in range(HALVES):
                        weigh(z_bank[j], "w3", j, aT_hi, aT_lo).then_inc(z_done, 1)
                    if k > 0:
                        pe.wait_ge(v_ready, half(p, k - 1, 1))
                    for j in range(HALVES):
                        weigh(v_bank[j], "w5", j, aT_hi, aT_lo, last=False)
                    pe.wait_ge(rh_lo_ready, half(p, k, 1))
                    for j in range(HALVES):
                        weigh(v_bank[j], "u5", j, rh_hi, rh_lo, first=False).then_inc(v_done, 1)
                    if k < UNITS - 1 or not last:
                        for j in range(HALVES):
                            adjacency(p, k + 1, j)
                if not last:
                    pe.wait_ge(z_ready, half(p, UNITS - 1, 1))
                    pe.wait_ge(v_ready, half(p, UNITS - 1, 1))

            with pe.Fori(0, PAIRS - 1) as p:
                pair(p, False)
            pair(PAIRS - 1, True)

        @block.scalar
        def _(act):
            def state_hi(p, k, s, j):
                nc.scalar.copy(hT_hi[s][:, j, :], hT[s][:, j, :]).then_inc(h_hi_ready, 1)

            def x_state_hi(p, s):
                act.wait_ge(hT_moved[s], x_moved(p))
                for j in range(HALVES):
                    state_hi(p, s, s, j)

            def new_rows(p, s):
                act.wait_ge(x_loaded[s], 16 * p + 16)
                for j in range(HALVES):
                    nc.scalar.copy(flat_half(nat_hi[s], j), flat_half(flat(x_in[s]), j)).then_inc(nat_hi_ready, 1)

            def a_high(p, k, j):
                act.wait_ge(a_done, half(p, k, j))
                nc.scalar.copy(aT_hi[:, j, :], ra_bank[j][:, :]).then_inc(a_hi_ready, 1)

            def load_table():
                nc.scalar.activation(table_scratch[:, :], table_scratch[:, :], ACT.Sigmoid)

            act.wait_ge(scratch_ready, 1)
            load_table()
            new_rows(0, 0)
            for q, (what, i, bank) in enumerate(PREP):
                if q == 4:
                    x_state_hi(0, 0)
                    a_high(0, 0, 0)
                act.wait_ge(prep_done, q + 1)
                dst = adjT_hi[:, i, :] if what == "adj" else flat(wT_hi[what])
                nc.scalar.copy(dst, banks[bank][:, :]).then_inc(prep_hi, 1)
            a_high(0, 0, 1)
            new_rows(0, 1)
            act.wait_ge(bias_ready, 3)
            act.wait_ge(prep_lo, len(PREP))

            def pair(p, last):
                def candidate(k):
                    for j in range(HALVES):
                        act.wait_ge(v_done, half(p, k, j))
                        nc.scalar.activation(v_sb[:, j, :], v_bank[j][:, :], ACT.Tanh,
                                             bias=bias[:, 2, j:j + 1]).then_inc(v_ready, 1)

                for k in range(UNITS):
                    s = k % SLOTS
                    for j in range(HALVES):
                        act.wait_ge(u_done, half(p, k, j))
                        nc.scalar.copy(u_sb[:, j, :], u_bank[j][:, :]).then_inc(u_copied, 1)
                    if 0 < k <= LAST_STEP:
                        for j in range(HALVES):
                            act.wait_ge(h_ready, half(p, k - 1, j))
                            state_hi(p, k + 1, 1 - s, j)
                    for j in range(HALVES):
                        act.wait_ge(r_summed, half(p, k, j))
                        nc.scalar.activation(r_sb[:, j, :], ra_bank[j][:, :], ACT.Sigmoid,
                                             bias=bias[:, 1, j:j + 1]).then_inc(r_ready, 1)
                    for j in range(HALVES):
                        act.wait_ge(rh_ready, half(p, k, j))
                        nc.scalar.copy(rh_hi[:, j, :], rh[:, j, :]).then_inc(rh_hi_ready, 1)
                    for j in range(HALVES):
                        act.wait_ge(z_summed, half(p, k, j))
                        nc.scalar.activation(z_sb[:, j, :], z_bank[j][:, :], ACT.Sigmoid,
                                             bias=bias[:, 0, j:j + 1]).then_inc(z_ready, 1)
                    if 0 < k <= LAST_STEP:
                        act.wait_ge(nat_moved[1 - s], moved(p, k - 1))
                        for j in range(HALVES):
                            nc.scalar.copy(by_quads(nat_hi[1 - s], j),
                                           nat_half(nat[1 - s], j)).then_inc(nat_hi_ready, 1)
                    if k == 0:
                        x_state_hi(p, 1)
                    if k >= LAST_STEP and not last:
                        new_rows(p + 1, k % SLOTS)
                    if k == UNITS - 1 and not last:
                        x_state_hi(p + 1, 0)
                    candidate(k)
                    if k < UNITS - 1 or not last:
                        for j in range(HALVES):
                            a_high(p, k + 1, j)

            with act.Fori(0, PAIRS - 1) as p:
                load_table()
                pair(p, False)
            pair(PAIRS - 1, True)

        @block.vector
        def _(dve):
            def new_rows_low(p, s):
                for j in range(HALVES):
                    dve.wait_ge(nat_hi_ready, half(p, s, j))
                    nc.vector.tensor_tensor(flat_half(nat_lo[s], j), flat_half(flat(x_in[s]), j),
                                            flat_half(nat_hi[s], j), ALU.subtract).then_inc(nat_lo_ready, 1)

            def transpose_x(p, s):
                dve.wait_ge(x_mixed_loaded[s], 16 * p + 16)
                for d in range(DT):
                    nc.vector.transpose(
                        x_blocks[s][:, :].rearrange("p (a d r t) -> p d a t r", a=QUADS, d=DT, t=NT)[:, d],
                        x_mixed[s][:, :, :].rearrange("p t (d i a) -> p d a t i", d=DT, a=QUADS)[:, d],
                    ).then_inc(x_blocks_ready, 1)

            def state_low(p, k, s):
                for j in range(HALVES):
                    dve.wait_ge(h_hi_ready, half(p, k, j))
                    nc.vector.tensor_tensor(hT_lo[s][:, j, :], hT[s][:, j, :], hT_hi[s][:, j, :],
                                            ALU.subtract).then_inc(h_lo_ready, 1)

            def a_low(p, k, j):
                dve.wait_ge(a_hi_ready, half(p, k, j))
                nc.vector.tensor_tensor(aT_lo[:, j, :], ra_bank[j][:, :], aT_hi[:, j, :],
                                        ALU.subtract).then_inc(a_lo_ready, 1)

            def prepare_low(q):
                what, i, bank = PREP[q]
                hi, lo = (adjT_hi[:, i, :], adjT_lo[:, i, :]) if what == "adj" else \
                    (flat(wT_hi[what]), flat(wT_lo[what]))
                dve.wait_ge(prep_hi, q + 1)
                nc.vector.tensor_tensor(lo, banks[bank][:, :], hi, ALU.subtract).then_inc(prep_lo, 1)

            transpose_x(0, 0)
            new_rows_low(0, 0)
            for q in range(4):
                prepare_low(q)
            for w, total in w_sum.items():
                dve.wait_ge(w_loaded[w], 16)
                nc.vector.tensor_tensor(total, w_in[w][:, :, 0:D], w_in[w][:, :, D:2 * D],
                                        ALU.add).then_inc(w_added, 1)
            transpose_x(0, 1)
            dve.wait_ge(bias_loaded, 16 * len(BIASES))
            for i, (a, b) in enumerate((("w3", "u3"), ("w4", "u3"), ("w5", "u5"))):
                nc.vector.tensor_tensor(bias[:, i, :], bias_in[:, BIASES.index(a), :],
                                        bias_in[:, BIASES.index(b), :], ALU.add).then_inc(bias_ready, 1)
            a_low(0, 0, 0)
            for q in range(4, len(PREP)):
                prepare_low(q)
            state_low(0, 0, 0)
            a_low(0, 0, 1)
            new_rows_low(0, 1)

            def pair(p, first, last):
                def update(k):
                    more = k < UNITS - 1 or not last
                    s = k % SLOTS

                    def diff(j):
                        dve.wait_ge(v_ready, half(p, k, j))
                        nc.vector.tensor_tensor(change[:, j, :], v_sb[:, j, :], hT[s][:, j, :],
                                                ALU.subtract).then_inc(diff_ready, 1)

                    def gate(j):
                        dve.wait_ge(diff_ready, half(p, k, j))
                        dve.wait_ge(z_ready, half(p, k, j))
                        nc.vector.tensor_tensor(change[:, j, :], z_sb[:, j, :], change[:, j, :],
                                                ALU.mult).then_inc(change_ready, 1)

                    def add(j):
                        dve.wait_ge(change_ready, half(p, k, j))
                        nc.vector.tensor_tensor(hT[s][:, j, :], hT[s][:, j, :], change[:, j, :],
                                                ALU.add).then_inc(h_ready, 1)

                    def blocks(j):
                        dve.wait_ge(h_ready, half(p, k, j))
                        nc.vector.transpose(
                            h_blocks[s][:, :].rearrange("p (b t d i) -> p d b t i", b=QUADS, t=NT, d=DT)[:, j],
                            hT[s][:, j, :].rearrange("p (t j b) -> p b t j", t=NT, b=QUADS),
                        ).then_inc(h_blocks_ready, 1)

                    diff(0)
                    gate(0)
                    diff(1)
                    add(0)
                    gate(1)
                    if not more:
                        blocks(0)
                    add(1)
                    if more:
                        a_low(p, k + 1, 0)
                        blocks(0)
                        a_low(p, k + 1, 1)
                    blocks(1)

                def residual(p, s):
                    dve.wait_ge(y_stored[s], stored(p))
                    dve.wait_ge(x_kept[s], 16 * p + 16)
                    dve.wait_ge(nat_moved[s], moved(p, LAST_STEP + s))
                    h_rows = nat[s][:, :].rearrange("p (a t d i) -> p t d a i", a=QUADS, t=NT, d=DT)
                    for t in range(NT):
                        x_row, y_row = (n[s][:, t, :].rearrange("p (d a i) -> p d a i", d=DT, a=QUADS)
                                        for n in (x_res, y))
                        nc.vector.tensor_tensor(y_row, h_rows[:, t], x_row, ALU.add).then_inc(y_summed, 1)

                def statistics(p, s):
                    for t in range(NT):
                        dve.wait_ge(y_summed, summed(p, s, t))
                        nc.vector.bn_stats(stats[s][:, t, :], y[s][:, t, :])
                    dve.drain()
                    for t in range(NT):
                        done = nc.vector.bn_aggr(moments[s][:, t, :], stats[s][:, t, :])
                    done.then_inc(moments_ready, 1)
                    dve.wait_ge(moments_ready, once(p, s))
                    nc.vector.tensor_scalar(var_eps[s][:, :], moments[s][:, :, 1], EPS, None,
                                            ALU.add).then_inc(var_ready, 1)

                def normalise(p, s):
                    dve.wait_ge(rstd_ready, once(p, s))
                    for t in range(NT):
                        done = nc.vector.tensor_scalar(y[s][:, t, :], y[s][:, t, :], moments[s][:, t, 0:1],
                                                       rstd[s][:, t:t + 1], ALU.subtract, ALU.mult)
                    done.then_inc(y_ready, 1)

                for k in range(UNITS):
                    s = k % SLOTS
                    if k == UNITS - 1:
                        finish = (p, 0)
                    elif k == 0 and not first:
                        finish = (p - 1, 1)
                    else:
                        finish = None
                    for j in range(HALVES):
                        dve.wait_ge(r_done, half(p, k, j))
                        dve.wait_ge(u_copied, half(p, k, j))
                        nc.vector.tensor_tensor(ra_bank[j][:, :], ra_bank[j][:, :], u_sb[:, j, :],
                                                ALU.add).then_inc(r_summed, 1)
                    for j in range(HALVES):
                        dve.wait_ge(r_ready, half(p, k, j))
                        nc.vector.tensor_tensor(rh[:, j, :], r_sb[:, j, :], hT[s][:, j, :],
                                                ALU.mult).then_inc(rh_ready, 1)
                    for j in range(HALVES):
                        dve.wait_ge(rh_hi_ready, half(p, k, j))
                        nc.vector.tensor_tensor(rh_lo[:, j, :], rh[:, j, :], rh_hi[:, j, :],
                                                ALU.subtract).then_inc(rh_lo_ready, 1)
                    for j in range(HALVES):
                        dve.wait_ge(z_done, half(p, k, j))
                        nc.vector.tensor_tensor(z_bank[j][:, :], z_bank[j][:, :], u_sb[:, j, :],
                                                ALU.add).then_inc(z_summed, 1)
                    if 0 < k <= LAST_STEP:
                        state_low(p, k + 1, 1 - s)
                        for j in range(HALVES):
                            dve.wait_ge(nat_hi_ready, half(p, k + 1, j))
                            nc.vector.tensor_tensor(by_quads(nat_lo[1 - s], j), nat_half(nat[1 - s], j),
                                                    by_quads(nat_hi[1 - s], j),
                                                    ALU.subtract).then_inc(nat_lo_ready, 1)
                    if finish:
                        residual(*finish)
                        statistics(*finish)
                    if k == 0:
                        state_low(p, 1, 1)
                    if k in (3, 4) and not last:
                        transpose_x(p + 1, k - 3)
                    if k >= LAST_STEP and not last:
                        new_rows_low(p + 1, k % SLOTS)
                    if k == UNITS - 1 and not last:
                        state_low(p, UNITS, 0)
                    update(k)
                    if finish:
                        normalise(*finish)
                if last:
                    residual(p, 1)
                    statistics(p, 1)
                    normalise(p, 1)

            pair(0, True, False)
            with dve.Fori(1, PAIRS - 1) as p:
                pair(p, False, False)
            pair(PAIRS - 1, False, True)


_INS = ['x', 'adj', 'L0_gnn_w3_w', 'L0_gnn_w3_b', 'L0_gnn_u3_w', 'L0_gnn_u3_b', 'L0_gnn_w4_w', 'L0_gnn_w4_b',
        'L0_gnn_w5_w', 'L0_gnn_w5_b', 'L0_gnn_u5_w', 'L0_gnn_u5_b']
_OUTS = [((16, 512, 256), 'float32')]


def kernel(**inputs):
    import numpy as _np
    import concourse.bacc as _bacc
    from concourse import mybir as _mybir
    from concourse.bass_utils import run_bass_kernel_spmd as _run

    nc = _bacc.Bacc("TRN2", target_bir_lowering=False, num_devices=1)
    arrays, args = {}, []
    for name in _INS:
        a = _np.ascontiguousarray(inputs[name])
        arrays[f"in_{name}_dram"] = a
        args.append(nc.dram_tensor(f"in_{name}_dram", a.shape, _mybir.dt.from_np(a.dtype), kind="ExternalInput").ap())
    for i, (shape, dtype) in enumerate(_OUTS):
        dt = _mybir.dt.from_np(_np.dtype(dtype))
        args.append(nc.dram_tensor(f"out_{i}_dram", shape, dt, kind="ExternalOutput").ap())
    gated_graph_steps_kernel(nc, *args)
    r = _run(nc, [arrays], core_ids=[0])
    return r.results[0]["out_0_dram"]
```

```python
from contextlib import ExitStack

import concourse.bass as bass
from concourse import mybir


def gated_graph_steps_kernel(nc: bass.Bass, x, adj, w3_w, w3_b, u3_w, u3_b, w4_w, w4_b,
                             w5_w, w5_b, u5_w, u5_b, out):
    F32 = mybir.dt.float32
    F32R = mybir.dt.float32r
    ALU = mybir.AluOpType
    ACT = mybir.ActivationFunctionType

    P = 128
    B, N, D = x.shape
    STEPS = 3
    SLOTS = 2
    PAIRS = B // SLOTS
    UNITS = STEPS * SLOTS
    NT = N // P
    DT = D // P
    HALVES = 2
    EPS = 1e-5
    WARM_UPS = 14
    LAST_STEP = UNITS - SLOTS
    NORMALISED_IN = (1, 2)
    QUAD = 32
    QUADS = P // QUAD
    MOVES = QUADS
    assert NT == QUADS and DT == HALVES and N == 512 and PAIRS >= 3

    def half(p, k, j):
        return 2 * UNITS * p + (2 * k + j + 1)

    def part(p, s, j):
        return 2 * SLOTS * p + (2 * s + j + 1)

    def once(p, s):
        return SLOTS * p + (s + 1)

    def summed(p, s, t):
        return SLOTS * NT * p + (NT * s + t + 1)

    def stored(p):
        return 16 * (p + 1)

    def moved(p, k):
        return 16 * MOVES * STEPS * p + 16 * MOVES * (k // SLOTS + 1)

    def x_moved(p):
        return 16 * MOVES * (p + 1)

    ctx = ExitStack()
    with ctx:
        def sb(name, shape, dt=F32):
            return ctx.enter_context(nc.sbuf_tensor(name, shape, dt))

        def sem(name):
            return ctx.enter_context(nc.semaphore(name))

        adjT_hi = sb("adjT_hi", [P, NT, N], F32R)
        adjT_lo = sb("adjT_lo", [P, NT, N], F32R)
        WEIGHTS = ("u3", "w4", "w3", "w5", "u5")
        wT_hi = {w: sb(f"{w}T_hi", [P, DT, D], F32R) for w in WEIGHTS}
        wT_lo = {w: sb(f"{w}T_lo", [P, DT, D], F32R) for w in WEIGHTS}
        BIASES = ("w3", "w4", "w5", "u3", "u5")
        bias_in = sb("bias_in", [P, len(BIASES), DT])
        bias = sb("bias", [P, 3, DT])
        ident = sb("ident", [P, P])
        minus_half = sb("minus_half", [P, NT])
        table_scratch = sb("table_scratch", [P, 1])

        x_in = [sb(f"x_in{s}", [P, NT, D]) for s in range(SLOTS)]
        x_mixed = [sb(f"x_mixed{s}", [P, NT, D]) for s in range(SLOTS)]
        x_res = [sb(f"x_res{s}", [P, NT, D]) for s in range(SLOTS)]
        x_blocks = [sb(f"x_blocks{s}", [P, NT * D]) for s in range(SLOTS)]
        h_blocks = [sb(f"h_blocks{s}", [P, NT * D]) for s in range(SLOTS)]
        nat = [sb(f"nat{s}", [P, NT * D]) for s in range(SLOTS)]
        nat_hi = [sb(f"nat_hi{s}", [P, NT * D], F32R) for s in range(SLOTS)]
        nat_lo = [sb(f"nat_lo{s}", [P, NT * D], F32R) for s in range(SLOTS)]
        hT = [sb(f"hT{s}", [P, DT, N]) for s in range(SLOTS)]
        hT_hi = [sb(f"hT_hi{s}", [P, DT, N], F32R) for s in range(SLOTS)]
        hT_lo = [sb(f"hT_lo{s}", [P, DT, N], F32R) for s in range(SLOTS)]
        y = [sb(f"y{s}", [P, NT, D]) for s in range(SLOTS)]
        stats = [sb(f"stats{s}", [P, NT, 6]) for s in range(SLOTS)]
        moments = [sb(f"moments{s}", [P, NT, 2]) for s in range(SLOTS)]
        var_eps = [sb(f"var_eps{s}", [P, NT]) for s in range(SLOTS)]
        rstd = [sb(f"rstd{s}", [P, NT]) for s in range(SLOTS)]
        minus_mean = sb("minus_mean", [P, NT])
        last_stats = sb("last_stats", [P, NT, HALVES, 6])

        aT_hi = sb("aT_hi", [P, DT, N], F32R)
        aT_lo = sb("aT_lo", [P, DT, N], F32R)
        u_sb = sb("u_sb", [P, DT, N])
        r_sb = sb("r_sb", [P, DT, N])
        z_sb = sb("z_sb", [P, DT, N])
        v_sb = sb("v_sb", [P, DT, N])
        rh = sb("rh", [P, DT, N])
        rh_hi = sb("rh_hi", [P, DT, N], F32R)
        rh_lo = sb("rh_lo", [P, DT, N], F32R)
        change = sb("change", [P, DT, N])

        old_product = x_mixed[1][:, :, :].rearrange("p (d t) i -> p d (t i)", d=DT)

        adj_in = sb("adj_in", [P, NT, N])
        w_in = {"w3": v_sb, "w4": r_sb, "w5": z_sb,
                "u3": change[:, 0, :].rearrange("p (t d) -> p t d", t=DT),
                "u5": change[:, 1, :].rearrange("p (t d) -> p t d", t=DT)}
        w_sum = {"w4": rh[:, 0, :].rearrange("p (t d) -> p t d", t=DT),
                 "w3": rh[:, 1, :].rearrange("p (t d) -> p t d", t=DT),
                 "w5": u_sb[:, 0, :].rearrange("p (t d) -> p t d", t=DT)}
        w_nat = {**w_sum, "u3": w_in["u3"], "u5": w_in["u5"]}

        banks = [ctx.enter_context(nc.psum_tensor(f"bank{i}", [P, N], F32)) for i in range(8)]
        u_bank, ra_bank, z_bank, v_bank = banks[0:2], banks[2:4], banks[4:6], banks[6:8]
        PREP = [("adj", 0, 4), ("adj", 1, 5), ("adj", 2, 6), ("adj", 3, 7),
                ("u3", 0, 4), ("w4", 0, 5), ("w3", 0, 6), ("w5", 0, 7), ("u5", 0, 2)]
        SPLIT = {what: q + 1 for q, (what, i, bank) in enumerate(PREP)}

        x_loaded = [sem(f"x_loaded{s}") for s in range(SLOTS)]
        x_mixed_loaded = [sem(f"x_mixed_loaded{s}") for s in range(SLOTS)]
        x_kept = [sem(f"x_kept{s}") for s in range(SLOTS)]
        hT_moved = [sem(f"hT_moved{s}") for s in range(SLOTS)]
        nat_moved = [sem(f"nat_moved{s}") for s in range(SLOTS)]
        y_stored = [sem(f"y_stored{s}") for s in range(SLOTS)]
        adj_loaded = [sem(f"adj_loaded{j}") for j in range(HALVES)]
        w_loaded = {w: sem(f"{w}_loaded") for w in WEIGHTS}
        bias_loaded = sem("bias_loaded")
        prep_done = sem("prep_done")
        x_transposed = sem("x_transposed")
        u_done = sem("u_done")
        r_done = sem("r_done")
        z_done = sem("z_done")
        v_done = sem("v_done")
        a_done = sem("a_done")
        last_transposed = sem("last_transposed")
        prep_hi = sem("prep_hi")
        u_copied = sem("u_copied")
        r_ready = sem("r_ready")
        z_ready = sem("z_ready")
        v_ready = sem("v_ready")
        last_y_centred = sem("last_y_centred")
        last_y0_ready = sem("last_y0_ready")
        rh_hi_ready = sem("rh_hi_ready")
        h_hi_ready = sem("h_hi_ready")
        nat_hi_ready = sem("nat_hi_ready")
        a_hi_ready = sem("a_hi_ready")
        w_added = sem("w_added")
        first_hT_ready = sem("first_hT_ready")
        prep_lo = sem("prep_lo")
        bias_ready = sem("bias_ready")
        r_summed = sem("r_summed")
        z_summed = sem("z_summed")
        rh_ready = sem("rh_ready")
        rh_lo_ready = sem("rh_lo_ready")
        diff_ready = sem("diff_ready")
        change_ready = sem("change_ready")
        h_ready = sem("h_ready")
        h_blocks_ready = sem("h_blocks_ready")
        x_blocks_ready = sem("x_blocks_ready")
        h_lo_ready = sem("h_lo_ready")
        nat_lo_ready = sem("nat_lo_ready")
        a_lo_ready = sem("a_lo_ready")
        moments_ready = sem("moments_ready")
        var_ready = sem("var_ready")
        y_ready = sem("y_ready")
        minus_mean_ready = sem("minus_mean_ready")
        new_part_ready = sem("new_part_ready")
        last_y_summed = sem("last_y_summed")
        last_y_ready = sem("last_y_ready")
        scratch_ready = sem("scratch_ready")
        ident_zero = sem("ident_zero")
        ident_ready = sem("ident_ready")
        exponent_ready = sem("exponent_ready")
        y_summed = sem("y_summed")
        old_product_ready = sem("old_product_ready")
        old_part_ready = sem("old_part_ready")
        rstd_ready = sem("rstd_ready")

        x_rows = x.rearrange("b (t p) d -> b p t d", p=P)
        x_mixed_rows = x.rearrange("b (p t) d -> b p t d", p=P)
        out_rows = out.rearrange("b (t p) d -> b p t d", p=P)

        HALF = NT * D // HALVES

        def flat_half(t, j):
            return t[:, j * HALF:(j + 1) * HALF]

        def by_quads(t, j):
            return t[:, :].rearrange("p (c a i) -> p a c i", a=QUADS, i=QUAD)[:, 2 * j:2 * j + 2]

        def nat_half(t, j):
            return t[:, :].rearrange("p (a c i) -> p a c i", a=QUADS, i=QUAD)[:, 2 * j:2 * j + 2]

        def residual_rows(s, t):
            h_rows = nat[s][:, :].rearrange("p (a t d i) -> p t d a i", a=QUADS, t=NT, d=DT)
            x_row, y_row = (n[s][:, t, :].rearrange("p (d a i) -> p d a i", d=DT, a=QUADS)
                            for n in (x_res, y))
            return y_row, h_rows[:, t], x_row

        def flat(t):
            return t[:, :, :].rearrange("p t d -> p (t d)")

        block = ctx.enter_context(nc.Block())

        @block.sync
        def _(sp):
            def move_h(p, k):
                s = k % SLOTS
                sp.wait_ge(h_blocks_ready, half(p, k, 1))
                for a in range(QUADS):
                    sp.dma_start(nat[s][:, a * D:(a + 1) * D],
                                 h_blocks[s][a * QUAD:(a + 1) * QUAD, :].rearrange("j (b x) -> j b x", b=QUADS)
                                 ).then_inc(nat_moved[s], 16)

            def move_x(p, s):
                sp.wait_ge(x_blocks_ready, part(p, s, 1))
                for q in range(QUADS):
                    sp.dma_start(hT[s][:, :, q * P:(q + 1) * P],
                                 x_blocks[s][q * QUAD:(q + 1) * QUAD, :].rearrange("i (a d n) -> i a d n",
                                                                                  a=QUADS, d=DT)
                                 ).then_inc(hT_moved[s], 16)

            adj_rows = adj.rearrange("(t p) m -> p t m", p=P)
            columns = N // HALVES
            sp.dma_start(adj_in[:, :, 0:columns], adj_rows[:, :, 0:columns]).then_inc(adj_loaded[0], 16)
            sp.dma_start(x_in[0][:, :, :], x_rows[0]).then_inc(x_loaded[0], 16)
            sp.dma_start(adj_in[:, :, columns:N], adj_rows[:, :, columns:N]).then_inc(adj_loaded[1], 16)
            for w, src in (("u3", u3_w), ("w4", w4_w), ("w3", w3_w), ("w5", w5_w), ("u5", u5_w)):
                sp.dma_start(w_in[w][:, :, :], src.rearrange("(t p) i -> p t i", p=P)).then_inc(w_loaded[w], 16)
            sp.dma_start(x_in[1][:, :, :], x_rows[1]).then_inc(x_loaded[1], 16)
            sp.dma_start(x_mixed[1][:, :, :], x_mixed_rows[1]).then_inc(x_mixed_loaded[1], 16)
            move_x(0, 1)

            def store(p, s):
                sp.wait_ge(y_ready, once(p, s))
                sp.dma_start(out_rows[SLOTS * p + s], y[s][:, :, :]).then_inc(y_stored[s], 16)

            def pair(p, first, last):
                for k in range(UNITS - 1 if last else UNITS):
                    move_h(p, k)
                    if k == 0:
                        if not first:
                            sp.wait_ge(y_summed, summed(p - 1, 1, NT - 1))
                        for s in range(SLOTS):
                            sp.wait_ge(x_loaded[s], 16 * p + 16)
                            sp.dma_start(x_res[s][:, :, :], x_in[s][:, :, :]).then_inc(x_kept[s], 16)
                    if k >= LAST_STEP and not last:
                        move_x(p + 1, k % SLOTS)
                    if k < LAST_STEP and not last:
                        if k == 0:
                            sp.wait_ge(nat_lo_ready, half(p, 1, 1))
                            sp.wait_ge(x_blocks_ready, part(p, 1, 1))
                            for s in range(SLOTS):
                                sp.wait_ge(x_kept[s], 16 * p + 16)
                        s = k % SLOTS
                        row = SLOTS * p + (SLOTS + s)
                        if k < SLOTS:
                            sp.dma_start(x_mixed[s][:, :, :], x_mixed_rows[row]).then_inc(x_mixed_loaded[s], 16)
                        else:
                            sp.dma_start(x_in[s][:, :, :], x_rows[row]).then_inc(x_loaded[s], 16)
                    if k in NORMALISED_IN and not first:
                        store(p - 1, NORMALISED_IN.index(k))

            pair(0, True, False)
            with sp.Fori(1, PAIRS - 1) as p:
                pair(p, False, False)
            pair(PAIRS - 1, False, True)
            sp.wait_ge(last_y0_ready, 1)
            sp.dma_start(out_rows[B - 2], y[0][:, :, :]).then_inc(y_stored[0], 16)
            for i in range(HALVES):
                tiles = slice(i * NT // HALVES, (i + 1) * NT // HALVES)
                sp.wait_ge(last_y_ready, i + 1)
                sp.dma_start(out_rows[B - 1][:, tiles, :], y[1][:, tiles, :]).then_inc(y_stored[1], 16)
            sp.wait_ge(y_stored[0], stored(PAIRS))
            sp.wait_ge(y_stored[1], stored(PAIRS) + 16)

        @block.gpsimd
        def _(pool):
            nc.gpsimd.memset(table_scratch[:, :], 0.0).then_inc(scratch_ready, 1)
            pool.sem_inc(x_mixed_loaded[0], 16)
            pool.sem_inc(x_blocks_ready, HALVES)
            pool.sem_inc(hT_moved[0], 16 * MOVES)
            for s in range(SLOTS):
                pool.sem_inc(y_stored[s], 16)
            nc.gpsimd.memset(ident[:, :], 0.0).then_inc(ident_zero, 1)
            pool.wait_ge(ident_zero, 1)
            nc.gpsimd.affine_select(out=ident[:, :], in_=ident[:, :], compare_op=ALU.not_equal, fill=1.0, base=0,
                                    pattern=[[-1, P]], channel_multiplier=1).then_inc(ident_ready, 1)
            pool.wait_ge(adj_loaded[1], 16)
            for i, src in enumerate((w3_b, w4_b, w5_b, u3_b, u5_b)):
                pool.dma_start(bias_in[:, i, :], src.rearrange("(t p) -> p t", p=P),
                               allow_slow_non_contiguous=True).then_inc(bias_loaded, 16)
            nc.gpsimd.memset(minus_half[:, :], -0.5).then_inc(exponent_ready, 1)
            pool.wait_ge(exponent_ready, 1)

            def residual(p, s):
                pool.wait_ge(y_stored[s], stored(p))
                pool.wait_ge(x_kept[s], 16 * p + 16)
                pool.wait_ge(nat_moved[s], moved(p, LAST_STEP + s))
                for t in range(NT):
                    nc.gpsimd.tensor_tensor(*residual_rows(s, t), ALU.add).then_inc(y_summed, 1)

            def inverse_deviation(p, s):
                pool.wait_ge(var_ready, once(p, s))
                nc.gpsimd.tensor_tensor(rstd[s][:, :], var_eps[s][:, :], minus_half[:, :],
                                        ALU.pow).then_inc(rstd_ready, 1)

            with pool.Fori(0, PAIRS - 1) as p:
                for s in range(SLOTS):
                    inverse_deviation(p, s)
            p = PAIRS - 1
            residual(p, 0)
            for j in range(HALVES):
                pool.wait_ge(z_ready, half(p, UNITS - 1, j))
                nc.gpsimd.tensor_tensor(old_product[:, j, :], z_sb[:, j, :], hT[1][:, j, :],
                                        ALU.mult).then_inc(old_product_ready, 1)
                pool.wait_ge(old_product_ready, j + 1)
                nc.gpsimd.tensor_tensor(hT[1][:, j, :], hT[1][:, j, :], old_product[:, j, :],
                                        ALU.subtract).then_inc(old_part_ready, 1)
            for s in range(SLOTS):
                inverse_deviation(p, s)

        @block.tensor
        def _(pe):
            def product(bank, w_hi, w_lo, m_hi, m_lo, first, last):
                nc.tensor.matmul(bank[:, :], w_hi, m_hi, start=first, stop=False)
                nc.tensor.matmul(bank[:, :], w_hi, m_lo, start=False, stop=False)
                return nc.tensor.matmul(bank[:, :], w_lo, m_hi, start=False, stop=last)

            def weigh(bank, w, j, m_hi, m_lo, first=True, last=True):
                for d in range(DT):
                    cols = slice(j * P, (j + 1) * P)
                    done = product(bank, wT_hi[w][:, d, cols], wT_lo[w][:, d, cols], m_hi[:, d, :], m_lo[:, d, :],
                                   first and d == 0, last and d == DT - 1)
                return done

            def adjacency(p, k, j, first=False):
                s = k % SLOTS
                if not first:
                    pe.wait_ge(r_ready, half(p, k - 1, j))
                for t in range(NT):
                    if j == 0 and first and t % (NT // HALVES) == 0:
                        pe.wait_ge(nat_lo_ready, half(p, k, t // (NT // HALVES)))
                    elif j == 0 and t == 0:
                        pe.wait_ge(nat_lo_ready, half(p, k, 1))
                    if j == 0 and first:
                        pe.wait_ge(prep_lo, t + 1)
                    hi, lo = (n[s][:, t * D + j * P:t * D + (j + 1) * P] for n in (nat_hi, nat_lo))
                    done = product(ra_bank[j], hi, lo, adjT_hi[:, t, :], adjT_lo[:, t, :], t == 0, t == NT - 1)
                done.then_inc(a_done, 1)

            def prepare(q):
                what, i, bank = PREP[q]
                if what == "adj":
                    tiles = [adj_in[:, t, i * P:(i + 1) * P] for t in range(NT)]
                else:
                    tiles = [w_nat[what][:, t, d * P:(d + 1) * P] for d in range(DT) for t in range(DT)]
                for n, tile in enumerate(tiles):
                    done = nc.tensor.transpose(banks[bank][:, n * P:(n + 1) * P], tile, ident[:, :])
                done.then_inc(prep_done, 1)

            pe.wait_ge(ident_ready, 1)
            for _ in range(WARM_UPS):
                nc.tensor.transpose(v_bank[0][:, 0:P], ident[:, :], ident[:, :])
            for q in range(NT):
                if q == NT // HALVES:
                    pe.wait_ge(x_loaded[0], 16)
                    for j in range(HALVES):
                        for t in range(NT):
                            done = nc.tensor.transpose(u_bank[j][:, t * P:(t + 1) * P],
                                                       x_in[0][:, t, j * P:(j + 1) * P], ident[:, :])
                        done.then_inc(x_transposed, 1)
                pe.wait_ge(adj_loaded[q // (NT // HALVES)], 16)
                prepare(q)
            for j in range(HALVES):
                adjacency(0, 0, j, first=True)
            for q in range(NT, len(PREP)):
                w = PREP[q][0]
                if w in w_sum:
                    pe.wait_ge(w_added, 1 + list(w_sum).index(w))
                else:
                    pe.wait_ge(w_loaded[w], 16)
                if w == PREP[-1][0]:
                    pe.wait_ge(a_lo_ready, half(0, 0, 0))
                prepare(q)
            pe.wait_ge(prep_lo, SPLIT["u3"])

            def pair(p, last):
                for k in range(UNITS):
                    s = k % SLOTS
                    pe.wait_ge(h_lo_ready, half(p, k, 1))
                    for j in range(HALVES):
                        weigh(u_bank[j], "u3", j, hT_hi[s], hT_lo[s]).then_inc(u_done, 1)
                    pe.wait_ge(a_lo_ready, half(p, k, 1))
                    if k == 0:
                        pe.wait_ge(prep_lo, len(PREP))
                    for j in range(HALVES):
                        weigh(ra_bank[j], "w4", j, aT_hi, aT_lo).then_inc(r_done, 1)
                    if k > 0:
                        pe.wait_ge(z_ready, half(p, k - 1, 1))
                    for j in range(HALVES):
                        weigh(z_bank[j], "w3", j, aT_hi, aT_lo).then_inc(z_done, 1)
                    if k > 0:
                        pe.wait_ge(v_ready, half(p, k - 1, 1))
                    for j in range(HALVES):
                        weigh(v_bank[j], "w5", j, aT_hi, aT_lo, last=False)
                    pe.wait_ge(rh_lo_ready, half(p, k, 1))
                    for j in range(HALVES):
                        weigh(v_bank[j], "u5", j, rh_hi, rh_lo, first=False).then_inc(v_done, 1)
                    if k < UNITS - 1 or not last:
                        for j in range(HALVES):
                            adjacency(p, k + 1, j)
                if last:
                    for j in range(HALVES):
                        pe.wait_ge(h_ready, half(p, UNITS - 1, j))
                        for t in range(NT):
                            done = nc.tensor.transpose(u_bank[j][:, t * P:(t + 1) * P],
                                                       hT[1][:, j, t * P:(t + 1) * P], ident[:, :])
                        done.then_inc(last_transposed, 1)
                else:
                    pe.wait_ge(z_ready, half(p, UNITS - 1, 1))
                    pe.wait_ge(v_ready, half(p, UNITS - 1, 1))

            with pe.Fori(0, PAIRS - 1) as p:
                pair(p, False)
            pair(PAIRS - 1, True)

        @block.scalar
        def _(act):
            def state_hi(p, k, s, j):
                nc.scalar.copy(hT_hi[s][:, j, :], hT[s][:, j, :]).then_inc(h_hi_ready, 1)

            def x_state_hi(p, s):
                act.wait_ge(hT_moved[s], x_moved(p))
                for j in range(HALVES):
                    state_hi(p, s, s, j)

            def new_rows(p, s):
                act.wait_ge(x_loaded[s], 16 * p + 16)
                for j in range(HALVES):
                    nc.scalar.copy(flat_half(nat_hi[s], j), flat_half(flat(x_in[s]), j)).then_inc(nat_hi_ready, 1)

            def a_high(p, k, j):
                act.wait_ge(a_done, half(p, k, j))
                nc.scalar.copy(aT_hi[:, j, :], ra_bank[j][:, :]).then_inc(a_hi_ready, 1)

            def load_table():
                nc.scalar.activation(table_scratch[:, :], table_scratch[:, :], ACT.Sigmoid)

            act.wait_ge(scratch_ready, 1)
            load_table()
            for q, (what, i, bank) in enumerate(PREP):
                if q == NT // HALVES:
                    new_rows(0, 0)
                if what == "u3":
                    for j in range(HALVES):
                        act.wait_ge(x_transposed, j + 1)
                        nc.scalar.copy(hT_hi[0][:, j, :], u_bank[j][:, :]).then_inc(h_hi_ready, 1)
                    a_high(0, 0, 0)
                    a_high(0, 0, 1)
                act.wait_ge(prep_done, q + 1)
                dst = adjT_hi[:, i, :] if what == "adj" else flat(wT_hi[what])
                nc.scalar.copy(dst, banks[bank][:, :]).then_inc(prep_hi, 1)
            act.wait_ge(prep_lo, len(PREP))

            def pair(p, last):
                def candidate(k):
                    for j in range(HALVES):
                        act.wait_ge(v_done, half(p, k, j))
                        nc.scalar.activation(v_sb[:, j, :], v_bank[j][:, :], ACT.Tanh,
                                             bias=bias[:, 2, j:j + 1]).then_inc(v_ready, 1)

                for k in range(UNITS):
                    s = k % SLOTS
                    for j in range(HALVES):
                        act.wait_ge(u_done, half(p, k, j))
                        nc.scalar.copy(u_sb[:, j, :], u_bank[j][:, :]).then_inc(u_copied, 1)
                    if 0 < k <= LAST_STEP:
                        for j in range(HALVES):
                            act.wait_ge(h_ready, half(p, k - 1, j))
                            state_hi(p, k + 1, 1 - s, j)
                    elif k == 0:
                        new_rows(p, 1)
                    elif not last:
                        new_rows(p + 1, 0)
                    for j in range(HALVES):
                        act.wait_ge(r_summed, half(p, k, j))
                        if k == 0 and j == 0:
                            act.wait_ge(bias_ready, 3)
                        nc.scalar.activation(r_sb[:, j, :], ra_bank[j][:, :], ACT.Sigmoid,
                                             bias=bias[:, 1, j:j + 1]).then_inc(r_ready, 1)
                    for j in range(HALVES):
                        act.wait_ge(rh_ready, half(p, k, j))
                        nc.scalar.copy(rh_hi[:, j, :], rh[:, j, :]).then_inc(rh_hi_ready, 1)
                    if 0 < k <= LAST_STEP:
                        act.wait_ge(nat_moved[1 - s], moved(p, k - 1))
                        for j in range(HALVES):
                            nc.scalar.copy(by_quads(nat_hi[1 - s], j),
                                           nat_half(nat[1 - s], j)).then_inc(nat_hi_ready, 1)
                    for j in range(HALVES):
                        act.wait_ge(z_summed, half(p, k, j))
                        nc.scalar.activation(z_sb[:, j, :], z_bank[j][:, :], ACT.Sigmoid,
                                             bias=bias[:, 0, j:j + 1]).then_inc(z_ready, 1)
                    if k == 0:
                        x_state_hi(p, 1)
                    if k == UNITS - 1 and not last:
                        x_state_hi(p + 1, 0)
                    candidate(k)
                    if k < UNITS - 1 or not last:
                        for j in range(HALVES):
                            a_high(p, k + 1, j)

            with act.Fori(0, PAIRS - 1) as p:
                load_table()
                pair(p, False)
            pair(PAIRS - 1, True)
            act.wait_ge(minus_mean_ready, 1)
            for t in range(NT):
                nc.scalar.activation(y[0][:, t, :], y[0][:, t, :], ACT.Identity,
                                     bias=minus_mean[:, t:t + 1]).then_inc(last_y_centred, 1)
            act.wait_ge(rstd_ready, once(PAIRS - 1, 0))
            for t in range(NT):
                act.wait_ge(last_y_centred, t + 1)
                done = nc.scalar.mul(y[0][:, t, :], y[0][:, t, :], rstd[0][:, t:t + 1])
            done.then_inc(last_y0_ready, 1)

        @block.vector
        def _(dve):
            def new_rows_low(p, s):
                for j in range(HALVES):
                    dve.wait_ge(nat_hi_ready, half(p, s, j))
                    nc.vector.tensor_tensor(flat_half(nat_lo[s], j), flat_half(flat(x_in[s]), j),
                                            flat_half(nat_hi[s], j), ALU.subtract).then_inc(nat_lo_ready, 1)

            def transpose_x(p, s):
                dve.wait_ge(x_mixed_loaded[s], 16 * p + 16)
                for d in range(DT):
                    nc.vector.transpose(
                        x_blocks[s][:, :].rearrange("p (a d r t) -> p d a t r", a=QUADS, d=DT, t=NT)[:, d],
                        x_mixed[s][:, :, :].rearrange("p t (d i a) -> p d a t i", d=DT, a=QUADS)[:, d],
                    ).then_inc(x_blocks_ready, 1)

            def state_low(p, k, s):
                for j in range(HALVES):
                    dve.wait_ge(h_hi_ready, half(p, k, j))
                    nc.vector.tensor_tensor(hT_lo[s][:, j, :], hT[s][:, j, :], hT_hi[s][:, j, :],
                                            ALU.subtract).then_inc(h_lo_ready, 1)

            def a_low(p, k, j):
                dve.wait_ge(a_hi_ready, half(p, k, j))
                nc.vector.tensor_tensor(aT_lo[:, j, :], ra_bank[j][:, :], aT_hi[:, j, :],
                                        ALU.subtract).then_inc(a_lo_ready, 1)

            def prepare_low(q):
                what, i, bank = PREP[q]
                hi, lo = (adjT_hi[:, i, :], adjT_lo[:, i, :]) if what == "adj" else \
                    (flat(wT_hi[what]), flat(wT_lo[what]))
                dve.wait_ge(prep_hi, q + 1)
                nc.vector.tensor_tensor(lo, banks[bank][:, :], hi, ALU.subtract).then_inc(prep_lo, 1)

            def add_weight_halves(w):
                dve.wait_ge(w_loaded[w], 16)
                nc.vector.tensor_tensor(w_sum[w], w_in[w][:, :, 0:D], w_in[w][:, :, D:2 * D],
                                        ALU.add).then_inc(w_added, 1)

            for q in range(NT):
                if q == NT // HALVES:
                    new_rows_low(0, 0)
                prepare_low(q)
            for j in range(HALVES):
                dve.wait_ge(h_hi_ready, half(0, 0, j))
                nc.vector.tensor_copy(hT[0][:, j, :], u_bank[j][:, :]).then_inc(first_hT_ready, 1)
                nc.vector.tensor_tensor(hT_lo[0][:, j, :], u_bank[j][:, :], hT_hi[0][:, j, :],
                                        ALU.subtract).then_inc(h_lo_ready, 1)
            add_weight_halves("w4")
            a_low(0, 0, 0)
            add_weight_halves("w3")
            add_weight_halves("w5")
            prepare_low(NT)
            a_low(0, 0, 1)
            for q in range(NT + 1, len(PREP)):
                prepare_low(q)
            dve.wait_ge(bias_loaded, 16 * len(BIASES))
            for i, (a, b) in enumerate((("w3", "u3"), ("w4", "u3"), ("w5", "u5"))):
                nc.vector.tensor_tensor(bias[:, i, :], bias_in[:, BIASES.index(a), :],
                                        bias_in[:, BIASES.index(b), :], ALU.add).then_inc(bias_ready, 1)
            transpose_x(0, 1)
            dve.wait_ge(first_hT_ready, HALVES)

            def pair(p, first, last):
                def update(k, between=None, after=None):
                    s = k % SLOTS

                    def diff(j):
                        dve.wait_ge(v_ready, half(p, k, j))
                        nc.vector.tensor_tensor(change[:, j, :], v_sb[:, j, :], hT[s][:, j, :],
                                                ALU.subtract).then_inc(diff_ready, 1)

                    def gate(j):
                        dve.wait_ge(diff_ready, half(p, k, j))
                        dve.wait_ge(z_ready, half(p, k, j))
                        nc.vector.tensor_tensor(change[:, j, :], z_sb[:, j, :], change[:, j, :],
                                                ALU.mult).then_inc(change_ready, 1)

                    def add(j):
                        dve.wait_ge(change_ready, half(p, k, j))
                        nc.vector.tensor_tensor(hT[s][:, j, :], hT[s][:, j, :], change[:, j, :],
                                                ALU.add).then_inc(h_ready, 1)

                    def blocks(j):
                        dve.wait_ge(h_ready, half(p, k, j))
                        nc.vector.transpose(
                            h_blocks[s][:, :].rearrange("p (b t d i) -> p d b t i", b=QUADS, t=NT, d=DT)[:, j],
                            hT[s][:, j, :].rearrange("p (t j b) -> p b t j", t=NT, b=QUADS),
                        ).then_inc(h_blocks_ready, 1)

                    diff(0)
                    gate(0)
                    diff(1)
                    add(0)
                    gate(1)
                    add(1)
                    a_low(p, k + 1, 0)
                    blocks(0)
                    if between:
                        between[0](*between[1:])
                    a_low(p, k + 1, 1)
                    blocks(1)
                    if after:
                        after[0](*after[1:])

                def residual(p, s):
                    dve.wait_ge(y_stored[s], stored(p))
                    dve.wait_ge(x_kept[s], 16 * p + 16)
                    dve.wait_ge(nat_moved[s], moved(p, LAST_STEP + s))
                    for t in range(NT):
                        nc.vector.tensor_tensor(*residual_rows(s, t), ALU.add).then_inc(y_summed, 1)

                def last_unit():
                    k, s = UNITS - 1, 1

                    def new_part(j):
                        dve.wait_ge(v_ready, half(p, k, j))
                        nc.vector.tensor_tensor(change[:, j, :], z_sb[:, j, :], v_sb[:, j, :],
                                                ALU.mult).then_inc(new_part_ready, 1)

                    def add(j):
                        dve.wait_ge(old_part_ready, j + 1)
                        dve.wait_ge(new_part_ready, j + 1)
                        nc.vector.tensor_tensor(hT[s][:, j, :], hT[s][:, j, :], change[:, j, :],
                                                ALU.add).then_inc(h_ready, 1)

                    def half_residual(j):
                        dve.wait_ge(last_transposed, j + 1)
                        feats = slice(j * P, (j + 1) * P)
                        nc.vector.tensor_tensor(y[s][:, :, feats],
                                                u_bank[j][:, :].rearrange("p (t i) -> p t i", t=NT),
                                                x_res[s][:, :, feats], ALU.add).then_inc(last_y_summed, 1)

                    def half_statistics(j):
                        dve.wait_ge(last_y_summed, j + 1)
                        for t in range(NT):
                            nc.vector.bn_stats(last_stats[:, t, j, :], y[s][:, t, j * P:(j + 1) * P])

                    new_part(0)
                    add(0)
                    new_part(1)
                    dve.wait_ge(y_stored[s], stored(p))
                    dve.wait_ge(x_kept[s], 16 * p + 16)
                    half_residual(0)
                    add(1)
                    half_statistics(0)
                    half_residual(1)
                    half_statistics(1)
                    dve.drain()
                    for t in range(NT):
                        done = nc.vector.bn_aggr(moments[s][:, t, :],
                                                 last_stats[:, t, :, :].rearrange("p j n -> p (j n)"))
                    done.then_inc(moments_ready, 1)
                    variance(p, s)
                    normalise_last(p, s)

                def variance(p, s):
                    dve.wait_ge(moments_ready, once(p, s))
                    nc.vector.tensor_scalar(var_eps[s][:, :], moments[s][:, :, 1], EPS, None,
                                            ALU.add).then_inc(var_ready, 1)

                def statistics(p, s):
                    for t in range(NT):
                        dve.wait_ge(y_summed, summed(p, s, t))
                        nc.vector.bn_stats(stats[s][:, t, :], y[s][:, t, :])
                    dve.drain()
                    for t in range(NT):
                        done = nc.vector.bn_aggr(moments[s][:, t, :], stats[s][:, t, :])
                    done.then_inc(moments_ready, 1)
                    variance(p, s)

                def normalise(p, s):
                    dve.wait_ge(rstd_ready, once(p, s))
                    for t in range(NT):
                        done = nc.vector.tensor_scalar(y[s][:, t, :], y[s][:, t, :], moments[s][:, t, 0:1],
                                                       rstd[s][:, t:t + 1], ALU.subtract, ALU.mult)
                    done.then_inc(y_ready, 1)

                def normalise_last(p, s):
                    dve.wait_ge(rstd_ready, once(p, s))
                    for t in range(NT):
                        done = nc.vector.tensor_scalar(y[s][:, t, :], y[s][:, t, :], moments[s][:, t, 0:1],
                                                       rstd[s][:, t:t + 1], ALU.subtract, ALU.mult)
                        if t % (NT // HALVES) == NT // HALVES - 1:
                            done.then_inc(last_y_ready, 1)

                between, after = {}, {}
                if not last:
                    between[UNITS - 1], after[UNITS - 1] = (residual, p, 0), (statistics, p, 0)
                if not first:
                    between[0], after[0] = (residual, p - 1, 1), (statistics, p - 1, 1)
                    for s in range(SLOTS):
                        between[NORMALISED_IN[s]] = (normalise, p - 1, s)

                for k in range(UNITS):
                    s = k % SLOTS
                    for j in range(HALVES):
                        dve.wait_ge(r_done, half(p, k, j))
                        dve.wait_ge(u_copied, half(p, k, j))
                        nc.vector.tensor_tensor(ra_bank[j][:, :], ra_bank[j][:, :], u_sb[:, j, :],
                                                ALU.add).then_inc(r_summed, 1)
                    for j in range(HALVES):
                        dve.wait_ge(r_ready, half(p, k, j))
                        nc.vector.tensor_tensor(rh[:, j, :], r_sb[:, j, :], hT[s][:, j, :],
                                                ALU.mult).then_inc(rh_ready, 1)
                    for j in range(HALVES):
                        dve.wait_ge(rh_hi_ready, half(p, k, j))
                        nc.vector.tensor_tensor(rh_lo[:, j, :], rh[:, j, :], rh_hi[:, j, :],
                                                ALU.subtract).then_inc(rh_lo_ready, 1)
                    for j in range(HALVES):
                        dve.wait_ge(z_done, half(p, k, j))
                        nc.vector.tensor_tensor(z_bank[j][:, :], z_bank[j][:, :], u_sb[:, j, :],
                                                ALU.add).then_inc(z_summed, 1)
                    if 0 < k <= LAST_STEP:
                        for j in range(HALVES):
                            dve.wait_ge(nat_hi_ready, half(p, k + 1, j))
                            nc.vector.tensor_tensor(by_quads(nat_lo[1 - s], j), nat_half(nat[1 - s], j),
                                                    by_quads(nat_hi[1 - s], j),
                                                    ALU.subtract).then_inc(nat_lo_ready, 1)
                        state_low(p, k + 1, 1 - s)
                    if k == 0:
                        new_rows_low(p, 1)
                        state_low(p, 1, 1)
                    if k in (3, 4) and not last:
                        transpose_x(p + 1, k - 3)
                    if k == UNITS - 1 and not last:
                        new_rows_low(p + 1, 0)
                        state_low(p, UNITS, 0)
                    if last and k == UNITS - 1:
                        statistics(p, 0)
                        nc.vector.tensor_scalar(minus_mean[:, :], moments[0][:, :, 0], -1.0, None,
                                                ALU.mult).then_inc(minus_mean_ready, 1)
                        last_unit()
                    else:
                        update(k, between.get(k), after.get(k))

            pair(0, True, False)
            with dve.Fori(1, PAIRS - 1) as p:
                pair(p, False, False)
            pair(PAIRS - 1, False, True)


_INS = ['x', 'adj', 'L0_gnn_w3_w', 'L0_gnn_w3_b', 'L0_gnn_u3_w', 'L0_gnn_u3_b', 'L0_gnn_w4_w', 'L0_gnn_w4_b',
        'L0_gnn_w5_w', 'L0_gnn_w5_b', 'L0_gnn_u5_w', 'L0_gnn_u5_b']
_OUTS = [((16, 512, 256), 'float32')]


def kernel(**inputs):
    import numpy as _np
    import concourse.bacc as _bacc
    from concourse import mybir as _mybir
    from concourse.bass_utils import run_bass_kernel_spmd as _run

    nc = _bacc.Bacc("TRN2", target_bir_lowering=False, num_devices=1)
    arrays, args = {}, []
    for name in _INS:
        a = _np.ascontiguousarray(inputs[name])
        arrays[f"in_{name}_dram"] = a
        args.append(nc.dram_tensor(f"in_{name}_dram", a.shape, _mybir.dt.from_np(a.dtype), kind="ExternalInput").ap())
    for i, (shape, dtype) in enumerate(_OUTS):
        dt = _mybir.dt.from_np(_np.dtype(dtype))
        args.append(nc.dram_tensor(f"out_{i}_dram", shape, dt, kind="ExternalOutput").ap())
    gated_graph_steps_kernel(nc, *args)
    r = _run(nc, [arrays], core_ids=[0])
    return r.results[0]["out_0_dram"]
```
